# Optimizing a Trainium2 kernel written in Bass

```python
import numpy as np
import jax
import jax.numpy as jnp

def _softmax(x, axis=-1):
    return jax.nn.softmax(x, axis=axis)

def _gelu(x):
    return jax.nn.gelu(x, approximate=True)

def _silu(x):
    return jax.nn.silu(x)

def _sigmoid(x):
    return jax.nn.sigmoid(x)

def _layernorm(x, axis=-1, eps=1e-05):
    m = jnp.mean(x, axis=axis, keepdims=True)
    v = jnp.var(x, axis=axis, keepdims=True)
    return (x - m) / jnp.sqrt(v + eps)

def _scatter_add(tgt, idx, src, axis=0):
    return tgt.at[idx].add(src)

def _segment_sum(src, seg, n):
    return jax.ops.segment_sum(src, seg, n)
kernel_name = 'mk_gnn_preln_d2_gnn_r8_b36beb'

def setup_inputs(seed: int=0):
    np.random.seed(seed)
    _w = jnp.asarray

    def _rec_inputs():
        import jax
        import jax.numpy as jnp
        _gk = jax.random.key(seed)
        x = -0.000202 + 1 * jax.random.normal(jax.random.fold_in(_gk, 1), (12500, 64), jnp.float32)
        src = jax.random.randint(jax.random.fold_in(_gk, 2), (400000,), 0, 12500, jnp.int32)
        dst = jnp.minimum((12500 * jax.random.uniform(jax.random.fold_in(_gk, 3), (400000,)) ** 2.0).astype(jnp.int32), 99999)
        _o = jnp.argsort(dst, stable=True)
        src = src[_o]
        dst = dst[_o]
        edge_attr_64 = 5.93493e-05 + 1.00006 * jax.random.normal(jax.random.fold_in(_gk, 11), (400000, 64), jnp.float32)
        return (x, src, dst, edge_attr_64)
    x, src, dst, edge_attr_64 = _rec_inputs()

    def _L0_gnn_setup():
        import jax, jax.numpy as jnp
        import numpy as np
        N_NODES = 12500
        N_EDGES = 150000
        D_NODE = 64
        D_EDGE = 64
        HIDDEN = 128
        EPS = 1e-05

        def _layer_norm(h, g, b):
            mu = jnp.mean(h, axis=-1, keepdims=True)
            var = jnp.mean(jnp.square(h - mu), axis=-1, keepdims=True)
            return (h - mu) * jax.lax.rsqrt(var + EPS) * g + b
        key = jax.random.key(seed)
        ks = jax.random.split(key, 10)
        d_in = D_NODE + D_EDGE
        s0 = 1.0 / np.sqrt(d_in)
        s1 = 1.0 / np.sqrt(HIDDEN)
        return {'x': jax.random.normal(ks[0], (N_NODES, D_NODE), dtype=jnp.float32), 'edge_index': jax.random.randint(ks[1], (2, N_EDGES), 0, N_NODES, dtype=jnp.int64), 'edge_attr': jax.random.normal(ks[2], (N_EDGES, D_EDGE), dtype=jnp.float32), 'W0': jax.random.uniform(ks[3], (d_in, HIDDEN), jnp.float32, -s0, s0), 'b0': jnp.zeros((HIDDEN,), jnp.float32), 'W1': jax.random.uniform(ks[4], (HIDDEN, HIDDEN), jnp.float32, -s1, s1), 'b1': jnp.zeros((HIDDEN,), jnp.float32), 'W2': jax.random.uniform(ks[5], (HIDDEN, D_NODE), jnp.float32, -s1, s1), 'b2': jnp.zeros((D_NODE,), jnp.float32), 'ln_g': jnp.ones((D_NODE,), jnp.float32), 'ln_b': jnp.zeros((D_NODE,), jnp.float32)}
    _L0_gnn_all = _L0_gnn_setup()
    _L0_gnn_in = {k: v for k, v in _L0_gnn_all.items() if k in ('W0', 'b0', 'W1', 'b1', 'W2', 'b2', 'ln_g', 'ln_b')}
    del _L0_gnn_all

    def _L1_gnn_setup():
        import jax, jax.numpy as jnp
        import numpy as np
        N_NODES = 12500
        N_EDGES = 125000
        D = 64

        def _glorot(key, shape):
            lim = 1.0 / np.sqrt(shape[0])
            return jax.random.uniform(key, shape, dtype=jnp.float32, minval=-lim, maxval=lim)

        def _sage_conv(h, src, dst, deg_inv, Wl, bl, Wr):
            agg = jax.ops.segment_sum(h[src], dst, num_segments=h.shape[0]) * deg_inv
            return agg @ Wl + bl + h @ Wr
        key = jax.random.key(seed)
        ks = jax.random.split(key, 12)
        x = jax.random.normal(ks[0], (N_NODES, D), dtype=jnp.float32)
        edge_index = jax.random.randint(ks[1], (2, N_EDGES), 0, N_NODES, dtype=jnp.int64)
        inp = {'x': x, 'edge_index': edge_index}
        names = ['W1l', 'b1', 'W1r', 'W2l', 'b2', 'W2r', 'W3l', 'b3', 'W3r']
        k = 2
        for i in range(3):
            inp[names[3 * i]] = _glorot(ks[k], (D, D))
            k += 1
            inp[names[3 * i + 1]] = jnp.zeros((D,), dtype=jnp.float32)
            inp[names[3 * i + 2]] = _glorot(ks[k], (D, D))
            k += 1
        return inp
    _L1_gnn_all = _L1_gnn_setup()
    _L1_gnn_in = {k: v for k, v in _L1_gnn_all.items() if k in ('W1l', 'b1', 'W1r', 'W2l', 'b2', 'W2r', 'W3l', 'b3', 'W3r')}
    del _L1_gnn_all
    return {'x': x, 'src': src, 'dst': dst, 'edge_attr_64': edge_attr_64, 'L0_gnn_W0': _L0_gnn_in['W0'], 'L0_gnn_b0': _L0_gnn_in['b0'], 'L0_gnn_W1': _L0_gnn_in['W1'], 'L0_gnn_b1': _L0_gnn_in['b1'], 'L0_gnn_W2': _L0_gnn_in['W2'], 'L0_gnn_b2': _L0_gnn_in['b2'], 'L0_gnn_ln_g': _L0_gnn_in['ln_g'], 'L0_gnn_ln_b': _L0_gnn_in['ln_b'], 'L1_gnn_W1l': _L1_gnn_in['W1l'], 'L1_gnn_b1': _L1_gnn_in['b1'], 'L1_gnn_W1r': _L1_gnn_in['W1r'], 'L1_gnn_W2l': _L1_gnn_in['W2l'], 'L1_gnn_b2': _L1_gnn_in['b2'], 'L1_gnn_W2r': _L1_gnn_in['W2r'], 'L1_gnn_W3l': _L1_gnn_in['W3l'], 'L1_gnn_b3': _L1_gnn_in['b3'], 'L1_gnn_W3r': _L1_gnn_in['W3r']}

def reference(x, src, dst, edge_attr_64, L0_gnn_W0, L0_gnn_b0, L0_gnn_W1, L0_gnn_b1, L0_gnn_W2, L0_gnn_b2, L0_gnn_ln_g, L0_gnn_ln_b, L1_gnn_W1l, L1_gnn_b1, L1_gnn_W1r, L1_gnn_W2l, L1_gnn_b2, L1_gnn_W2r, L1_gnn_W3l, L1_gnn_b3, L1_gnn_W3r):
    import jax
    import jax.numpy as jnp

    def _L0_gnn_ref(x, edge_index, edge_attr, W0, b0, W1, b1, W2, b2, ln_g, ln_b):
        import jax, jax.numpy as jnp
        import numpy as np
        N_NODES = 12500
        N_EDGES = 150000
        D_NODE = 64
        D_EDGE = 64
        HIDDEN = 128
        EPS = 1e-05

        def _layer_norm(h, g, b):
            mu = jnp.mean(h, axis=-1, keepdims=True)
            var = jnp.mean(jnp.square(h - mu), axis=-1, keepdims=True)
            return (h - mu) * jax.lax.rsqrt(var + EPS) * g + b
        col = edge_index[1]
        agg = jax.ops.segment_sum(edge_attr, col, num_segments=N_NODES)
        h = jnp.concatenate([x, agg], axis=-1)
        h = jax.nn.relu(h @ W0 + b0)
        h = jax.nn.relu(h @ W1 + b1)
        h = h @ W2 + b2
        h = _layer_norm(h, ln_g, ln_b)
        return h + x

    def _L1_gnn_ref(x, edge_index, W1l, b1, W1r, W2l, b2, W2r, W3l, b3, W3r):
        import jax, jax.numpy as jnp
        import numpy as np
        N_NODES = 12500
        N_EDGES = 125000
        D = 64

        def _glorot(key, shape):
            lim = 1.0 / np.sqrt(shape[0])
            return jax.random.uniform(key, shape, dtype=jnp.float32, minval=-lim, maxval=lim)

        def _sage_conv(h, src, dst, deg_inv, Wl, bl, Wr):
            agg = jax.ops.segment_sum(h[src], dst, num_segments=h.shape[0]) * deg_inv
            return agg @ Wl + bl + h @ Wr
        src, dst = (edge_index[0], edge_index[1])
        n = x.shape[0]
        deg = jax.ops.segment_sum(jnp.ones((src.shape[0],), dtype=x.dtype), dst, num_segments=n)
        deg_inv = (1.0 / jnp.maximum(deg, 1.0))[:, None]
        h = jax.nn.relu(_sage_conv(x, src, dst, deg_inv, W1l, b1, W1r))
        h = jax.nn.relu(_sage_conv(h, src, dst, deg_inv, W2l, b2, W2r))
        return _sage_conv(h, src, dst, deg_inv, W3l, b3, W3r)
    edge_index = jnp.stack([src, dst])
    h = jnp.maximum(_layernorm(x, axis=-1), 0.0)
    x = x + _L0_gnn_ref(h, edge_index, edge_attr_64, L0_gnn_W0, L0_gnn_b0, L0_gnn_W1, L0_gnn_b1, L0_gnn_W2, L0_gnn_b2, L0_gnn_ln_g, L0_gnn_ln_b)
    h = jnp.maximum(_layernorm(x, axis=-1), 0.0)
    x = x + _L1_gnn_ref(h, edge_index, L1_gnn_W1l, L1_gnn_b1, L1_gnn_W1r, L1_gnn_W2l, L1_gnn_b2, L1_gnn_W2r, L1_gnn_W3l, L1_gnn_b3, L1_gnn_W3r)
    return x

_drawn_inputs = setup_inputs


def setup_inputs(seed=0):
    import zlib

    import numpy as np

    out = dict(_drawn_inputs(seed))
    spreads = {'L0_gnn_b0': (0.0, 0.322),
     'L0_gnn_b1': (0.0, 0.1),
     'L0_gnn_b2': (0.0, 0.1),
     'L0_gnn_ln_g': (1.0, 0.2),
     'L0_gnn_ln_b': (0.0, 0.1),
     'L1_gnn_b1': (0.0, 0.785),
     'L1_gnn_b2': (0.0, 0.291),
     'L1_gnn_b3': (0.0, 0.1)}
    factors = {}
    for name, (base, spread) in spreads.items():
        noise = np.random.default_rng([zlib.crc32(name.encode()), seed]).standard_normal(out[name].shape)
        drawn = base * np.exp(spread * noise) if base else spread * noise
        out[name] = jnp.asarray(drawn.astype(out[name].dtype))
    for name, factor in factors.items():
        out[name] = (out[name] * factor).astype(out[name].dtype)
    return out
```

```python
from contextlib import ExitStack

import numpy as np

import concourse.bass as bass
from concourse import mybir

F32 = mybir.dt.float32
I32 = mybir.dt.int32
ALU = mybir.AluOpType
ACT = mybir.ActivationFunctionType
AX = mybir.AxisListType.X

P = 128
D = 64
HID = 128
EPS = 1e-5
T = 5
GE = T * P
BG = 5
NSLOT = 5
BODY = BG * NSLOT
WIN = 64
OH_SLOTS = 5
PS_SLOTS = 5
CP, J = 125, 4
CH = CP * J
LAG = 2


def gnn_kernel(nc, x, src, dst, edge_attr, W0, b0, W1, b1, W2, b2, ln_g, ln_b,
               W1l, c1, W1r, W2l, c2, W2r, W3l, c3, W3r, out):
    N = x.shape[0]
    E = src.shape[0]
    NG = E // GE
    Q = max(q for q in range(1, P + 1) if NG % q == 0)
    S = NG // Q
    NC = N // CH
    NR = NC * J
    NIT = NG // BODY
    NWIN = -(-N // WIN)
    WIDE = (NWIN + 1) * WIN
    assert N % CH == 0 and E % GE == 0 and NG % BODY == 0 and S * GE <= NSLOT * BG * T * D

    with ExitStack() as ctx:
        def sb(name, shape, dt=F32):
            return ctx.enter_context(nc.sbuf_tensor(name, shape, dt))

        def sem(name):
            return ctx.enter_context(nc.semaphore(name))

        agg_h = sb("agg_h", [P, WIDE])
        nodes = sb("nodes", [P, max(2 * NR * D, WIDE)])
        xrows = nodes[0:CP, 0:NR * D]
        hrows = nodes[0:CP, NR * D:2 * NR * D]
        deg = nodes[0:D, 0:WIDE]
        ring = sb("ring", [P, NSLOT * BG * T * D])
        rel = sb("rel", [P, NG * T])
        src_idx = sb("src_idx", [P, NG * T], I32)
        idx = sb("idx", [P, NSLOT, BG * T], I32)
        onehot = sb("onehot", [P, OH_SLOTS, T, WIN])
        iota = sb("iota", [P, WIN])
        iota_run = sb("iota_run", [P, WIN])
        ident = sb("ident", [P, P])
        ones = sb("ones", [P, P])
        bases = sb("bases", [1, NG // BG, 8], I32)
        base_f = sb("base_f", [P, S])
        base_i = sb("base_i", [P, S], I32)
        span = sb("span", [P, S])
        top_f = sb("top_f", [P, 1])
        flag_f = sb("flag_f", [1, 2])
        flag_b = sb("flag_b", [P, 1])
        flag = sb("flag", [1, 1], I32)
        w0 = sb("w0", [P, HID])
        w1 = sb("w1", [HID, HID])
        w2 = sb("w2", [HID, D])
        wc = sb("wc", [P, 3, D])
        bias = sb("bias", [HID, 4])
        brow = sb("brow", [P, 4, D])
        eps = sb("eps", [P, 1])
        stat = sb("stat", [P, 3, NR])
        hid = sb("hid", [P, 2, 2, CH])
        stage = sb("stage", [P, 2, J * D])
        resid = sb("resid", [P, 2, J * D])
        ps = [ctx.enter_context(nc.psum_tensor(f"ps{i}", [P, 512], F32)) for i in range(8)]

        base_dram = nc.dram_tensor("base_dram", [NG], I32).ap()
        tables = [nc.dram_tensor(f"h_table{i}", [N, D], F32).ap() for i in range(3)]
        x1_dram = nc.dram_tensor("x1_dram", [N, D], F32).ap()

        s_dstf = sem("s_dstf")
        s_relrow = sem("s_relrow")
        s_srcrow = sem("s_srcrow")
        s_top = sem("s_top")
        s_w = sem("s_w")
        s_x = sem("s_x")
        s_dst = sem("s_dst")
        s_src = sem("s_src")
        s_go = sem("s_go")
        s_const = sem("s_const")
        s_eps = sem("s_eps")
        s_rel = sem("s_rel")
        s_rel_out = sem("s_rel_out")
        s_idx_t = sem("s_idx_t")
        s_idx_out = sem("s_idx_out")
        s_based = sem("s_based")
        s_base_st = sem("s_base_st")
        s_base_ld = sem("s_base_ld")
        s_flag_t = sem("s_flag_t")
        s_flag_w = sem("s_flag_w")
        s_flag_b = sem("s_flag_b")
        s_flag = sem("s_flag")
        s_dv = sem("s_dv")
        s_sq_in = sem("s_sq_in")
        s_sq = sem("s_sq")
        s_var = sem("s_var")
        s_root = sem("s_root")
        s_h = sem("s_h")
        s_ht = sem("s_ht")
        s_hc = sem("s_hc")
        s_resid = sem("s_resid")
        s_zero = sem("s_zero")
        s_attr = [sem(f"s_attr{i}") for i in range(NSLOT)]
        s_rows = [sem(f"s_rows{i}") for i in range(NSLOT)]
        s_idx = sem("s_idx")
        s_oh = sem("s_oh")
        s_mm = sem("s_mm")
        s_add = sem("s_add")
        s_dadd = sem("s_dadd")
        s_pass = sem("s_pass")
        w_row = sem("w_row")
        w_rows = sem("w_rows")
        w_iota = sem("w_iota")
        w_dadd = sem("w_dadd")
        w_idx = sem("w_idx")
        w_oh = sem("w_oh")
        w_mm = sem("w_mm")
        w_add = sem("w_add")
        s_m1 = sem("s_m1")
        s_a1 = sem("s_a1")
        s_m2 = sem("s_m2")
        s_a2 = sem("s_a2")
        s_m3 = sem("s_m3")
        s_y = sem("s_y")
        s_x1 = sem("s_x1")
        s_x1_st = sem("s_x1_st")
        s_tab = [sem(f"s_tab{i}") for i in range(3)]
        s_scaled = sem("s_scaled")
        s_conv = sem("s_conv")
        s_act = sem("s_act")
        s_tp = sem("s_tp")
        s_stage = sem("s_stage")
        s_store = [sem("s_store0"), sem("s_store1")]
        s_res = [sem("s_res0"), sem("s_res1")]
        s_o = sem("s_o")

        cidx = lambda k: slice(k * CH, (k + 1) * CH)

        def column(rows, k, j):
            return agg_h[rows, k * CH + j:(k + 1) * CH:J]

        def table_chunk(t, k):
            return t[k * CH:(k + 1) * CH, :].rearrange("(p j) f -> p (j f)", j=J)

        attr_v = edge_attr.rearrange("(b g p t) f -> b p g (t f)", g=BG, p=P, t=T)
        ring_v = ring[:].rearrange("p (s g r) -> p s g r", s=NSLOT, g=BG)
        tile_of = ring[:].rearrange("p (n t f) -> p n t f", t=T, f=D)
        irow = ring[0:Q, 0:S * GE]
        frow = agg_h[0:Q, 0:S * GE]
        irow_i = irow.bitcast(I32)
        rel_v = rel[:].rearrange("p (q s t) -> p s t q", s=S, t=T)
        src_v = src_idx[:].rearrange("p (q s t) -> p s t q", s=S, t=T)
        STS = [(s, t) for s in range(S) for t in range(T)]
        yrows = ring[0:CP, 0:NR * D]
        sq = agg_h[0:CP, 0:NR * D]
        rows3 = lambda a: a.rearrange("p (r f) -> p r f", f=D)
        wide = lambda a: a.unsqueeze(2).to_broadcast([CP, NR, D])
        feat = lambda i: brow[0:CP, i:i + 1, :].to_broadcast([CP, NR, D])

        def load_attr(sp, s, batch):
            sp.dma_start(ring_v[:, s, :, :],
                         attr_v[bass.ds(batch, 1)].rearrange("o p g r -> (o p) g r")).then_inc(s_attr[s], 16)

        def store_out(sp, k):
            n = 2 * NC + k
            sp.wait_ge(s_o, k + 1)
            sp.dma_start(table_chunk(out, k), stage[0:CP, n % 2, :]).then_inc(s_store[n % 2], 16)

        def stored(eng, n):
            if n >= 2:
                eng.wait_ge(s_store[n % 2], 16 * (n // 2))

        def copy_h(act, n):
            for k in range(NC):
                act.wait_ge(s_ht, n * NC + k + 1)
                nc.scalar.copy(agg_h[D:2 * D, cidx(k)].rearrange("f (p j) -> f j p", j=J),
                               ps[4 + k % 2][0:D, 0:CH].rearrange("f (j p) -> f j p", j=J)).then_inc(s_hc, 1)

        def transpose_h(pe, n):
            pe.wait_ge(s_h, n + 1)
            for k in range(NC):
                if k >= 2:
                    pe.wait_ge(s_hc, n * NC + k - 1)
                for j in range(J):
                    r = k * J + j
                    last = nc.tensor.transpose(ps[4 + k % 2][0:D, j * CP:(j + 1) * CP], hrows[:, r * D:(r + 1) * D],
                                               ident[0:CP, 0:CP])
                last.then_inc(s_ht, 1)

        def after_conv(dve, layer, k, output_rows, own):
            if layer == 2:
                output_rows(k)
            else:
                dve.wait_ge(s_conv, layer * NC + k + 1)
                own(nc.vector.memset(agg_h[0:D, cidx(k)], 0.0))

        block = ctx.enter_context(nc.Block())

        @block.sync
        def _(sp):
            sp.dma_start(irow_i, dst.rearrange("(q n) -> q n", q=Q)).then_inc(s_dst, 16)
            sp.dma_start(xrows.rearrange("p (k r) -> p k r", k=NC),
                         x.rearrange("(k p j) f -> p k (j f)", p=CP, j=J)).then_inc(s_x, 16)
            sp.dma_start(w0[0:D, :], W0[D:2 * D, :]).then_inc(s_w, 16)
            sp.dma_start(w0[D:2 * D, :], W0[0:D, :]).then_inc(s_w, 16)
            sp.dma_start(w1[:], W1).then_inc(s_w, 16)
            sp.dma_start(w2[:], W2).then_inc(s_w, 16)
            for i, (wl, wr) in enumerate(((W1l, W1r), (W2l, W2r), (W3l, W3r))):
                sp.dma_start(wc[0:D, i, :], wl).then_inc(s_w, 16)
                sp.dma_start(wc[D:2 * D, i, :], wr).then_inc(s_w, 16)
            for i, b in enumerate((b0, b1, c1, c2)):
                sp.dma_start(bias[0:b.shape[0], i:i + 1], b.rearrange("(p o) -> p o", o=1)).then_inc(s_w, 16)
            for i, b in enumerate((b2, ln_g, ln_b, c3)):
                sp.dma_start(brow[:, i, :], b.rearrange("(o f) -> o f", o=1).to_broadcast([P, D])).then_inc(s_w, 16)
            sp.wait_ge(s_dstf, 1)
            sp.dma_start(irow_i, src.rearrange("(q n) -> q n", q=Q)).then_inc(s_src, 16)
            sp.wait_ge(s_based, 1)
            sp.dma_start(base_dram.rearrange("(q s) -> q s", q=Q), base_i[0:Q, :]).then_inc(s_base_st, 16)
            sp.wait_ge(s_base_st, 16)
            sp.dma_start(bases[:, :, 0:BG], base_dram.rearrange("(o c g) -> o c g", o=1, g=BG)).then_inc(s_base_ld, 16)

            sp.wait_ge(s_flag, 1)
            sp.wait_ge(s_srcrow, 1)
            covered = sp.value_load(flag[0:1, 0:1], min_val=0, max_val=1)
            with sp.If(covered == 1):
                for s in range(NSLOT):
                    load_attr(sp, s, s)
                with sp.Fori(1, NIT) as i:
                    for s in range(NSLOT):
                        sp.wait_ge(s_mm, ((i - 1) * NSLOT + (s + 1)) * BG)
                        load_attr(sp, s, i * NSLOT + s)
            with sp.Else():
                with sp.Fori(0, NG) as g:
                    sp.wait_ge(w_add, g * NWIN + 1)
                    sp.dma_start(ring_v[:, 0, 0, :], edge_attr.rearrange("(g p t) f -> g p (t f)", p=P, t=T)[bass.ds(g, 1)].rearrange("o p r -> (o p) r")).then_inc(w_row, 16)

            sp.wait_ge(s_h, 2)
            sp.dma_start(tables[0].rearrange("(k p j) f -> p k (j f)", p=CP, j=J),
                         hrows.rearrange("p (k r) -> p k r", k=NC)).then_inc(s_tab[0], 16)
            sp.wait_ge(s_x1, 1)
            sp.dma_start(x1_dram.rearrange("(k p j) f -> p k (j f)", p=CP, j=J),
                         yrows.rearrange("p (k r) -> p k r", k=NC)).then_inc(s_x1_st, 16)
            for layer in range(2):
                for k in range(NC):
                    n = layer * NC + k
                    sp.wait_ge(s_stage, n + 1)
                    sp.dma_start(table_chunk(tables[layer + 1], k), stage[0:CP, n % 2, :]).then_inc(s_store[n % 2], 16)
            sp.wait_ge(s_x1_st, 16)
            for k in range(NC):
                if k >= 2:
                    sp.wait_ge(s_o, k - 1)
                sp.dma_start(resid[0:CP, k % 2, :], table_chunk(x1_dram, k)).then_inc(s_res[k % 2], 16)
                if k >= 1:
                    store_out(sp, k - 1)
            store_out(sp, NC - 1)
            for b in range(2):
                sp.wait_ge(s_store[b], 16 * len([n for n in range(3 * NC) if n % 2 == b]))

        @block.gpsimd
        def _(pool):
            nc.gpsimd.memset(ident[:], 0.0).then_inc(s_const, 1)
            nc.gpsimd.iota(iota[:], pattern=[[1, WIN]], base=0, channel_multiplier=0,
                           allow_small_or_imprecise_dtypes=True).then_inc(s_const, 1)
            nc.gpsimd.memset(ones[:], 1.0).then_inc(s_const, 1)
            nc.gpsimd.memset(eps[:], EPS).then_inc(s_const, 1)
            pool.wait_ge(s_const, 4)
            nc.gpsimd.affine_select(out=ident[:], in_=ident[:], compare_op=ALU.not_equal, fill=1.0, base=0,
                                    pattern=[[-1, P]], channel_multiplier=1).then_inc(s_const, 1)
            pool.wait_ge(s_h, 1)
            pool.wait_ge(s_w, 16 * 18)
            nc.gpsimd.tensor_tensor(xrows, xrows, hrows, ALU.add).then_inc(s_resid, 1)
            pool.wait_ge(s_resid, 1)
            nc.gpsimd.tensor_tensor(rows3(xrows), rows3(xrows), feat(2), ALU.add).then_inc(s_resid, 1)
            pool.wait_ge(s_sq_in, 3)
            nc.gpsimd.tensor_tensor(rows3(yrows), rows3(yrows), feat(3), ALU.add).then_inc(s_x1, 1)
            pool.wait_ge(s_x1_st, 16)
            pool.wait_ge(s_flag, 1)
            covered = pool.value_load(flag[0:1, 0:1], min_val=0, max_val=1)
            for layer in range(3):
                if layer == 0:
                    pool.wait_ge(s_tab[0], 16)
                else:
                    for b in range(2):
                        pool.wait_ge(s_store[b], 16 * len([n for n in range(layer * NC) if n % 2 == b]))
                table = tables[layer]

                def gather(slot, c, landed):
                    nc.gpsimd.indirect_dma_start(
                        out=ring[:, (slot * BG * T + c) * D:(slot * BG * T + c + 1) * D], out_offset=None, in_=table,
                        in_offset=bass.IndirectOffsetOnAxis(ap=idx[:, slot, c:c + 1], axis=0)).then_inc(landed, 16)

                with pool.If(covered == 1):
                    with pool.Fori(0, NIT) as i:
                        for s in range(NSLOT):
                            pool.wait_ge(s_idx, (layer * NIT + i) * NSLOT + (s + 1))
                            pool.wait_ge(s_mm, (((layer + 1) * NIT + i - 1) * NSLOT + (s + 1)) * BG)
                            pool.sem_inc(s_go, 1)
                            for c in range(BG * T):
                                gather(s, c, s_rows[s])
                with pool.Else():
                    with pool.Fori(0, NG) as g:
                        pool.wait_ge(w_idx, layer * NG + g + 1)
                        pool.wait_ge(w_add, ((layer + 1) * NG + g) * NWIN + 1)
                        pool.sem_inc(s_go, 1)
                        for c in range(T):
                            gather(0, c, w_rows)

        @block.scalar
        def _(act):
            def layernorm_roots(n):
                act.wait_ge(s_sq_in, n + 1)
                nc.scalar.activation(sq, hrows if n != 1 else yrows, ACT.Square).then_inc(s_sq, 1)
                act.wait_ge(s_var, n + 1)
                nc.scalar.activation(stat[0:CP, 2, :], stat[0:CP, 1, :], ACT.Sqrt, bias=eps[0:CP, :],
                                     scale=1.0 / D).then_inc(s_root, 1)

            act.wait_ge(s_const, 5)
            layernorm_roots(0)
            copy_h(act, 0)
            act.wait_ge(s_idx_out, len(STS))
            act.wait_ge(s_flag, 1)
            covered = act.value_load(flag[0:1, 0:1], min_val=0, max_val=1)
            act.wait_ge(s_w, 16 * 18)
            for step in range(NC + 1):
                if step < NC:
                    k = step
                    act.wait_ge(s_m1, k + 1)
                    if k >= 2:
                        act.wait_ge(s_m2, k - 1)
                    nc.scalar.activation(hid[:, 0, k % 2, :], ps[k % 2][:, 0:CH], ACT.Relu, bias=bias[:, 0:1]).then_inc(s_a1, 1)
                if step >= 1:
                    k = step - 1
                    act.wait_ge(s_m2, k + 1)
                    if k >= 2:
                        act.wait_ge(s_m3, k - 1)
                    nc.scalar.activation(hid[:, 1, k % 2, :], ps[2 + k % 2][:, 0:CH], ACT.Relu, bias=bias[:, 1:2]).then_inc(s_a2, 1)
            layernorm_roots(1)
            layernorm_roots(2)
            copy_h(act, 1)
            for layer in range(3):
                with act.If(covered == 1):
                    with act.Fori(0, NIT) as i:
                        for s in range(NSLOT):
                            act.wait_ge(s_mm, (((layer + 1) * NIT + i - 1) * NSLOT + (s + 1)) * BG)
                            nc.scalar.copy(idx[:, s, :], src_idx[:, bass.ds((i * NSLOT + s) * (BG * T), BG * T)]).then_inc(s_idx, 1)
                with act.Else():
                    with act.Fori(0, NG) as g:
                        act.wait_ge(w_add, ((layer + 1) * NG + g) * NWIN + 1)
                        nc.scalar.copy(idx[:, 0, 0:T], src_idx[:, bass.ds(g * T, T)]).then_inc(w_idx, 1)
                if layer == 2:
                    break
                for k in range(NC):
                    n = layer * NC + k
                    act.wait_ge(s_conv, n + 1)
                    nc.scalar.activation(agg_h[D:2 * D, cidx(k)], ps[k % 2][0:D, 0:CH], ACT.Relu,
                                         bias=bias[0:D, 2 + layer:3 + layer]).then_inc(s_act, 1)
                    act.wait_ge(s_tp, n + 1)
                    stored(act, n)
                    nc.scalar.copy(stage[0:CP, n % 2, :], ps[2 + k % 2][0:CP, 0:J * D]).then_inc(s_stage, 1)

        @block.tensor
        def _(pe):
            pe.wait_ge(s_const, 5)
            pe.wait_ge(s_top, 1)
            nc.tensor.transpose(ps[2][0:1, 0:Q], top_f[0:Q, 0:1], ident[0:Q, 0:Q]).then_inc(s_flag_t, 1)
            pe.wait_ge(s_flag_w, 1)
            nc.tensor.matmul(ps[3][0:Q, 0:1], ones[0:1, 0:Q], flag_f[0:1, 1:2], start=True, stop=True).then_inc(s_flag_b, 1)
            for row, done, out_sem in ((s_relrow, s_rel, s_rel_out), (s_srcrow, s_idx_t, s_idx_out)):
                pe.wait_ge(row, 1)
                for n, (s, t) in enumerate(STS):
                    if n >= 2:
                        pe.wait_ge(out_sem, n - 1)
                    nc.tensor.transpose(ps[n % 2][:, 0:Q], frow[:, s * GE + t:(s + 1) * GE:T], ident[0:Q, 0:Q]).then_inc(done, 1)
            transpose_h(pe, 0)
            pe.wait_ge(s_flag, 1)
            covered = pe.value_load(flag[0:1, 0:1], min_val=0, max_val=1)

            def window(tiles, oh, bank, with_deg, done):
                for t in range(T):
                    last = nc.tensor.matmul(ps[bank][0:D, 0:WIN], tiles[:, t, :], onehot[:, oh, t, :],
                                            start=(t == 0), stop=(t == T - 1))
                if with_deg:
                    for t in range(T):
                        last = nc.tensor.matmul(ps[bank][0:D, WIN:2 * WIN], ones[:, 0:D], onehot[:, oh, t, :],
                                                start=(t == 0), stop=(t == T - 1))
                last.then_inc(done, 1)

            def segment_pass(n):
                with pe.If(covered == 1):
                    with pe.Fori(0, NIT) as i:
                        for s in range(NSLOT):
                            if n == 0:
                                pe.wait_ge(s_attr[s], (i + 1) * 16)
                            else:
                                pe.wait_ge(s_rows[s], (i + 1 + (n - 1) * NIT) * (16 * BG * T))
                            for g in range(BG):
                                m = s * BG + g
                                pe.wait_ge(s_oh, (i + n * NIT) * BODY + (m + 1))
                                window(tile_of[:, m], m % OH_SLOTS, m % PS_SLOTS, n == 1, s_mm)
                with pe.Else():
                    with pe.Fori(0, NG) as g:
                        with pe.Fori(0, NWIN) as k:
                            if n == 0:
                                pe.wait_ge(w_row, (g + 1) * 16)
                            else:
                                pe.wait_ge(w_rows, (g + 1 + (n - 1) * NG) * (16 * T))
                            pe.wait_ge(w_oh, (g + n * NG) * NWIN + k + 1)
                            window(tile_of[:, 0], 0, 0, n == 1, w_mm)

            pe.wait_ge(s_hc, NC)
            segment_pass(0)
            pe.wait_ge(s_pass, 1)
            pe.wait_ge(s_w, 16 * 18)
            for step in range(NC + 2):
                if step < NC:
                    k = step
                    if k >= 2:
                        pe.wait_ge(s_a1, k - 1)
                    nc.tensor.matmul(ps[k % 2][:, 0:CH], w0[:], agg_h[:, cidx(k)], start=True, stop=True).then_inc(s_m1, 1)
                if 1 <= step <= NC:
                    k = step - 1
                    pe.wait_ge(s_a1, k + 1)
                    if k >= 2:
                        pe.wait_ge(s_a2, k - 1)
                    nc.tensor.matmul(ps[2 + k % 2][:, 0:CH], w1[:], hid[:, 0, k % 2, :], start=True, stop=True).then_inc(s_m2, 1)
                if step >= 2:
                    k = step - 2
                    pe.wait_ge(s_a2, k + 1)
                    if k >= 2:
                        pe.wait_ge(s_y, k - 1)
                    for j in range(J):
                        last = nc.tensor.matmul(ps[4 + k % 2][0:CP, j * D:(j + 1) * D], hid[:, 1, k % 2, j:CH:J], w2[:],
                                                start=True, stop=True)
                    last.then_inc(s_m3, 1)
            transpose_h(pe, 1)
            pe.wait_ge(s_hc, 2 * NC)
            for layer in range(3):
                segment_pass(layer + 1)
                if layer == 2:
                    break

                def to_rows(k):
                    n = layer * NC + k
                    pe.wait_ge(s_act, n + 1)
                    if n >= 2:
                        pe.wait_ge(s_stage, n - 1)
                    for j in range(J):
                        last = nc.tensor.transpose(ps[2 + k % 2][0:CP, j * D:(j + 1) * D], column(slice(D, 2 * D), k, j),
                                                   ident[D:2 * D, D:2 * D])
                    last.then_inc(s_tp, 1)

                for k in range(NC):
                    n = layer * NC + k
                    pe.wait_ge(s_scaled, n + 1)
                    if n >= 2:
                        pe.wait_ge(s_act, n - 1)
                    nc.tensor.matmul(ps[k % 2][0:D, 0:CH], wc[:, layer, :], agg_h[:, cidx(k)], start=True, stop=True).then_inc(s_conv, 1)
                    if k >= 1:
                        to_rows(k - 1)
                to_rows(NC - 1)
                pe.wait_ge(s_stage, (layer + 1) * NC)
            for k in range(NC):
                pe.wait_ge(s_scaled, 2 * NC + k + 1)
                if k >= 2:
                    pe.wait_ge(s_o, k - 1)
                for j in range(J):
                    last = nc.tensor.matmul(ps[k % 2][0:CP, j * D:(j + 1) * D], column(slice(0, P), k, j), wc[:, 2, :],
                                            start=True, stop=True)
                last.then_inc(s_conv, 1)

        @block.vector
        def _(dve):
            steps = [0]

            def own(ins):
                steps[0] += 1
                ins.then_inc(s_dv, 1)
                dve.wait_ge(s_dv, steps[0])

            v = nc.vector
            dve.wait_ge(s_dst, 16)
            v.tensor_copy(frow, irow_i).then_inc(s_dstf, 1)
            dve.wait_ge(s_dstf, 1)
            dve.wait_ge(s_const, 5)
            groups = frow.rearrange("q (s e) -> q s e", e=GE)
            own(v.tensor_reduce(base_f[0:Q, :], groups, AX, ALU.min))
            own(v.tensor_reduce(span[0:Q, :], groups, AX, ALU.max))
            own(v.tensor_tensor(span[0:Q, :], span[0:Q, :], base_f[0:Q, :], ALU.subtract))
            v.tensor_reduce(top_f[0:Q, 0:1], span[0:Q, :], AX, ALU.max).then_inc(s_top, 1)
            dve.wait_ge(s_flag_t, 1)
            own(v.tensor_reduce(flag_f[0:1, 0:1], ps[2][0:1, 0:Q], AX, ALU.max))
            v.tensor_scalar(flag_f[0:1, 1:2], flag_f[0:1, 0:1], float(WIN), None, ALU.is_lt).then_inc(s_flag_w, 1)
            dve.wait_ge(s_flag_b, 1)
            own(v.tensor_copy(flag_b[0:Q, :], ps[3][0:Q, 0:1]))
            own(v.tensor_scalar(base_f[0:Q, :], base_f[0:Q, :], flag_b[0:Q, 0:1], None, ALU.mult))
            v.tensor_copy(base_i[0:Q, :], base_f[0:Q, :]).then_inc(s_based, 1)
            for s in range(S):
                ins = v.tensor_scalar(groups[:, s, :], groups[:, s, :], base_f[0:Q, s:s + 1], None, ALU.subtract)
            ins.then_inc(s_relrow, 1)
            for n, (s, t) in enumerate(STS):
                dve.wait_ge(s_rel, n + 1)
                v.tensor_copy(rel_v[:, s, t, :], ps[n % 2][:, 0:Q]).then_inc(s_rel_out, 1)
            dve.wait_ge(s_src, 16)
            v.tensor_copy(frow, irow_i).then_inc(s_srcrow, 1)
            for n, (s, t) in enumerate(STS):
                dve.wait_ge(s_idx_t, n + 1)
                v.tensor_copy(src_v[:, s, t, :], ps[n % 2][:, 0:Q]).then_inc(s_idx_out, 1)
            dve.wait_ge(s_idx_out, len(STS))
            dve.wait_ge(s_base_ld, 16)
            v.tensor_copy(iota_run[:], iota[:]).then_inc(w_iota, 1)
            v.tensor_copy(flag[:], flag_f[0:1, 1:2]).then_inc(s_flag, 1)

            def centre(n, rows, centred):
                own(v.tensor_reduce(stat[0:CP, 0, :], rows3(rows), AX, ALU.add))
                own(v.tensor_scalar(stat[0:CP, 0, :], stat[0:CP, 0, :], 1.0 / D, None, ALU.mult))
                v.tensor_tensor(rows3(centred), rows3(rows), wide(stat[0:CP, 0, :]), ALU.subtract).then_inc(s_sq_in, 1)
                dve.wait_ge(s_sq, n + 1)
                v.tensor_reduce(stat[0:CP, 1, :], rows3(sq), AX, ALU.add).then_inc(s_var, 1)
                dve.wait_ge(s_root, n + 1)
                own(v.reciprocal(stat[0:CP, 2, :], stat[0:CP, 2, :]))

            def normed_relu():
                v.scalar_tensor_tensor(out=rows3(hrows), in0=rows3(hrows), scalar=0.0, in1=wide(stat[0:CP, 2, :]),
                                       op0=ALU.max, op1=ALU.mult).then_inc(s_h, 1)

            dve.wait_ge(s_x, 16)
            centre(0, xrows, hrows)
            normed_relu()
            own(v.memset(agg_h[0:D, :], 0.0))
            dve.sem_inc(s_add, 1)
            dve.sem_inc(w_add, 1)
            covered = dve.value_load(flag[0:1, 0:1], min_val=0, max_val=1)

            def segment_pass(n):
                with_deg = n == 1

                def one_hot(m, first, numbers, done):
                    v.tensor_tensor(onehot[:, m % OH_SLOTS, :, :], numbers[:, :].unsqueeze(1).to_broadcast([P, T, WIN]),
                                    rel[:, bass.ds(first, T)].unsqueeze(2).to_broadcast([P, T, WIN]),
                                    ALU.is_equal).then_inc(done, 1)

                def add(to, m, at, col, done):
                    v.tensor_tensor(to[0:D, bass.ds(at, WIN)], to[0:D, bass.ds(at, WIN)],
                                    ps[m % PS_SLOTS][0:D, col:col + WIN], ALU.add).then_inc(done, 1)

                with dve.If(covered == 1):
                    with dve.Fori(0, NIT) as i:
                        base = {}
                        for m in range(BODY + LAG):
                            if m < BODY:
                                one_hot(m, (i * BODY + m) * T, iota, s_oh)
                            if m < LAG:
                                continue
                            a = m - LAG
                            if a % BG == 0:
                                _, base = nc.values_load_multi_w_load_instructions(bases[0:1, bass.ds(i * NSLOT + a // BG, 1), 0:BG].rearrange("o c g -> o (c g)"),
                                                      engines=[mybir.EngineType.DVE], min_val=0, max_val=N - 1,
                                                      skip_runtime_bounds_check_because="a base is one of dst")
                            dve.wait_ge(s_mm, (i + n * NIT) * BODY + (a + 1))
                            dve.wait_ge(s_add, (i + n * NIT) * BODY + (a + 1))
                            add(agg_h, a, base[a % BG], 0, s_add)
                            if with_deg:
                                dve.wait_ge(s_dadd, i * BODY + (a + 1))
                                add(deg, a, base[a % BG], WIN, s_dadd)
                    dve.wait_ge(s_add, (n + 1) * NG + 1)
                    if with_deg:
                        dve.wait_ge(s_dadd, NG + 1)
                with dve.Else():
                    with dve.Fori(0, NG) as g:
                        dve.wait_ge(w_iota, (g + n * NG) * (NWIN + 1) + 1)
                        v.tensor_copy(iota_run[:], iota[:]).then_inc(w_iota, 1)
                        with dve.Fori(0, NWIN) as k:
                            at = (g + n * NG) * NWIN + k
                            dve.wait_ge(w_iota, (g + n * NG) * (NWIN + 1) + k + 2)
                            one_hot(0, g * T, iota_run, w_oh)
                            dve.wait_ge(w_mm, at + 1)
                            dve.wait_ge(w_add, at + 1)
                            add(agg_h, 0, k * WIN, 0, w_add)
                            if with_deg:
                                dve.wait_ge(w_dadd, g * NWIN + k + 1)
                                add(deg, 0, k * WIN, WIN, w_dadd)
                            dve.wait_ge(w_oh, at + 1)
                            v.tensor_scalar(iota_run[:], iota_run[:], float(WIN), None, ALU.add).then_inc(w_iota, 1)
                    dve.wait_ge(w_add, (n + 1) * NG * NWIN + 1)
                    if with_deg:
                        dve.wait_ge(w_dadd, NG * NWIN + 1)

            segment_pass(0)
            dve.sem_inc(s_pass, 1)
            dve.wait_ge(s_w, 16 * 18)
            for k in range(NC):
                dve.wait_ge(s_m3, k + 1)
                v.tensor_tensor(yrows[:, k * J * D:(k + 1) * J * D].rearrange("p (j f) -> p j f", f=D),
                                ps[4 + k % 2][0:CP, 0:J * D].rearrange("p (j f) -> p j f", f=D),
                                brow[0:CP, 0:1, :].to_broadcast([CP, J, D]), ALU.add).then_inc(s_y, 1)
            dve.wait_ge(s_y, NC)
            centre(1, yrows, yrows)
            own(v.tensor_tensor(rows3(yrows), rows3(yrows), wide(stat[0:CP, 2, :]), ALU.mult))
            own(v.tensor_tensor(rows3(yrows), rows3(yrows), feat(1), ALU.mult))
            dve.wait_ge(s_resid, 2)
            own(v.tensor_tensor(yrows, yrows, xrows, ALU.add))
            dve.wait_ge(s_ht, NC)
            centre(2, yrows, hrows)
            normed_relu()
            own(v.memset(agg_h[0:D, :], 0.0))
            dve.wait_ge(s_tab[0], 16)
            dve.wait_ge(s_ht, 2 * NC)
            own(v.memset(deg, 0.0))
            dve.sem_inc(s_dadd, 1)
            dve.sem_inc(w_dadd, 1)

            def output_rows(k):
                n = 2 * NC + k
                dve.wait_ge(s_conv, n + 1)
                dve.wait_ge(s_res[k % 2], 16 * (k // 2 + 1))
                stored(dve, n)
                v.tensor_tensor(stage[0:CP, n % 2, :], ps[k % 2][0:CP, 0:J * D], resid[0:CP, k % 2, :], ALU.add).then_inc(s_o, 1)

            for layer in range(3):
                segment_pass(layer + 1)
                for k in range(NC):
                    if layer == 0:
                        own(v.tensor_scalar(deg[:, cidx(k)], deg[:, cidx(k)], 1.0, None, ALU.max))
                        own(v.reciprocal(deg[:, cidx(k)], deg[:, cidx(k)]))
                    v.tensor_tensor(agg_h[0:D, cidx(k)], agg_h[0:D, cidx(k)], deg[:, cidx(k)], ALU.mult).then_inc(s_scaled, 1)
                    if k >= 1:
                        after_conv(dve, layer, k - 1, output_rows, own)
                after_conv(dve, layer, NC - 1, output_rows, own)

_INS = ['x', 'src', 'dst', 'edge_attr_64', 'L0_gnn_W0', 'L0_gnn_b0', 'L0_gnn_W1', 'L0_gnn_b1', 'L0_gnn_W2', 'L0_gnn_b2',
        'L0_gnn_ln_g', 'L0_gnn_ln_b', 'L1_gnn_W1l', 'L1_gnn_b1', 'L1_gnn_W1r', 'L1_gnn_W2l', 'L1_gnn_b2', 'L1_gnn_W2r',
        'L1_gnn_W3l', 'L1_gnn_b3', 'L1_gnn_W3r']


def kernel(**inputs):
    import concourse.bacc as bacc
    from concourse.bass_utils import run_bass_kernel_spmd

    nc = bacc.Bacc("TRN2", target_bir_lowering=False, num_devices=1)
    arrays, args = {}, []
    for name in _INS:
        a = np.ascontiguousarray(inputs[name])
        arrays[f"in_{name}"] = a
        args.append(nc.dram_tensor(f"in_{name}", a.shape, mybir.dt.from_np(a.dtype), kind="ExternalInput").ap())
    args.append(nc.dram_tensor("out_x", inputs['x'].shape, F32, kind="ExternalOutput").ap())
    gnn_kernel(nc, *args)
    r = run_bass_kernel_spmd(nc, [arrays], core_ids=[0])
    return r.results[0]["out_x"]
```

```python
from contextlib import ExitStack
from math import ceil, sqrt

import numpy as np

import concourse.bass as bass
from concourse import mybir

F32 = mybir.dt.float32
BF16 = mybir.dt.bfloat16
F16 = mybir.dt.float16
I32 = mybir.dt.int32
ALU = mybir.AluOpType
ACT = mybir.ActivationFunctionType
AX = mybir.AxisListType.X

P = 128
D = 64
HID = 128
EPS = 1e-5
T = 5
GE = T * P
BG = 5
RING = 5
BODY = 25
WIN = 64
OH_SLOTS = 5
LAG = 2
CP, J = 125, 4
CH = CP * J
COLS = 128
GSLOT = 4
MAX_BLOCKS = 82
ROUND = 12582912.0


class Region:

    def __init__(self, k, w, units, first_tile, first_block, first_unit, first_quantum, first_base):
        self.k, self.w, self.units, self.pairs = k, w, units, 0
        self.first_tile, self.first_block, self.first_unit = first_tile, first_block, first_unit
        self.first_quantum, self.first_base = first_quantum, first_base
        self.padded = 4 * ceil(units / 4)
        half = ceil(w / 2)
        self.quanta = [half] if half <= 5 else [ceil(half / 2), half - ceil(half / 2)]
        assert w % 2 == 0 and half <= 10

    tiles = property(lambda self: 2 * self.pairs * self.units * self.k)
    blocks = property(lambda self: 2 * self.pairs)


def plan(n_nodes, n_edges):
    n_tiles = n_edges // P
    regions, t, b, u, q, s = [], 0, 0, 0, 0, 0
    while True:
        k = 2
        w, end = 2, t
        while True:
            w += 2
            units = COLS // w
            end = t + 2 * units * k
            pos = end / n_tiles
            per_tile = 2 * P * n_nodes * pos / n_edges
            if 1 + per_tile * k + 5 * sqrt(per_tile * k * n_nodes * 2 * pos / n_edges) <= w:
                break
        if (n_tiles - end) / T < 2 * (b + 2) + 6 or b + 4 > MAX_BLOCKS:
            units = max(x for x in range(units) if (n_tiles - t - 2 * x * k) % T == 0
                        and (n_tiles - t - 2 * x * k) / T >= (2 * (b + 2) + 3 if x else 2 * b + 3))
            if units:
                regions.append(Region(k, w, units, t, b, u, q, s))
                regions[-1].pairs = 1
            return regions
        if not regions or (regions[-1].k, regions[-1].w) != (k, w):
            regions.append(Region(k, w, units, t, b, u, q, s))
        r = regions[-1]
        r.pairs += 1
        t, b, u = end, b + 2, u + 2 * units
        q += 2 * units * len(r.quanta)
        s += 2 * r.padded


def gnn_kernel(nc, x, src, dst, edge_attr, W0, b0, W1, b1, W2, b2, ln_g, ln_b,
               W1l, c1, W1r, W2l, c2, W2r, W3l, c3, W3r, out):
    N = x.shape[0]
    E = src.shape[0]
    NT = E // P
    NG = E // GE
    Q = max(q for q in range(1, P + 1) if NG % q == 0)
    S = NG // Q
    TR = S * T
    NC = N // CH
    NR = NC * J
    NIT = NG // BODY
    NWIN = -(-N // WIN)
    WIDE = (NWIN + COLS // WIN) * WIN
    RE = TR * P

    regions = plan(N, E)
    last = regions[-1]
    TD = last.first_tile + last.tiles
    NB = last.first_block + last.blocks
    NU = last.first_unit + last.blocks * last.units
    NQ = last.first_quantum + last.blocks * last.units * len(last.quanta)
    NBASE = last.first_base + last.blocks * last.padded
    G = (NT - TD) // T
    BBASE = NBASE + 4 * ceil(G / 4)
    ALL_BASES = BBASE + NB
    PAIRED = 2 * NB
    REST4 = (G - PAIRED - 3) // 4
    REST = PAIRED + 4 * REST4
    WMAX = max(r.w for r in regions)
    KW = max(r.k * r.w for r in regions)
    KMAX = max(r.k for r in regions)
    assert N % CH == 0 and E % GE == 0 and NG % BODY == 0 and (NT - TD) % T == 0 and G >= PAIRED + 3
    assert WMAX * NR <= 2048 and KMAX * P <= 256 and 2 * (NU + G + NG + NB) <= NR * D
    OHB = KW * NR + KMAX * P
    slot_uses = [len(range(s, G, GSLOT)) for s in range(GSLOT)]

    with ExitStack() as ctx:
        def sb(name, shape, dt=F32):
            return ctx.enter_context(nc.sbuf_tensor(name, shape, dt))

        def sem(name):
            return ctx.enter_context(nc.semaphore(name))

        agg_h = sb("agg_h", [P, max(WIDE, 3 * RE, NR * D)])
        NRD = NR * D
        CB = COLS * NR // 2
        big = sb("big", [P, max(2 * CB + 3 * NRD // 2, 3 * NRD + 4 * CH, max(WIDE, 2 * NRD) + RING * T * D, 2 * NRD + 3 * RE,
                                2 * NRD + RING * T * D)])
        hrows = big[0:CP, 0:NRD]
        xrows = big[0:CP, NRD:2 * NRD]
        yrows = big[0:CP, 2 * NRD:3 * NRD]
        hid_v = big[:, 3 * NRD:3 * NRD + 4 * CH].rearrange("p (l s c) -> p l s c", l=2, s=2)
        deg = big[0:1, 0:WIDE]
        rat = max(WIDE, 2 * NRD)
        ring = big[:, rat:rat + RING * T * D].rearrange("p (s r) -> p s r", s=RING)
        counts = [big[0:CP, i * CB:(i + 1) * CB].bitcast(BF16).rearrange("p (d a) -> p d a", a=NR) for i in range(2)]
        parts = big[0:CP, 2 * CB:2 * CB + 3 * NRD // 2].bitcast(BF16).rearrange("p (a s f) -> p a s f", s=3, f=D)
        key = sb("key", [P, NT])
        who = sb("who", [P, NT])
        scratch = sb("scratch", [P, max(NT, OHB, 5 * J * D)])
        rel0 = scratch[:, 0:NT]
        unit_oh = [scratch[:, i * OHB // 2:(i + 1) * OHB // 2].bitcast(BF16) for i in range(2)]
        chunk_rows = scratch[:, 0:5 * J * D].rearrange("p (i r) -> p i r", i=5)
        stage, resid, pool_left = chunk_rows[:, 0:2, :], chunk_rows[:, 2:4, :], chunk_rows[:, 4, :]
        gring = sb("gring", [P, GSLOT, T, D])
        idx = sb("idx", [P, GSLOT, T], I32)
        onehot = sb("onehot", [P, OH_SLOTS, T, WIN])
        iota = sb("iota", [P, WIN])
        iota_run = sb("iota_run", [P, WIN])
        iota16 = sb("iota16", [P, max(P, WMAX * NR)], F16)
        ident = sb("ident", [P, P])
        ones = sb("ones", [P, P])
        ones16 = sb("ones16", [P, 1], BF16)
        bases = sb("bases", [1, max((NG // BG) * 8, ALL_BASES)], I32)
        base0 = bases[:, 0:(NG // BG) * 8].rearrange("o (c g) -> o c g", g=8)
        ubase = bases[:, 0:NBASE]
        gbase = bases[:, NBASE:NBASE + 4 * ceil(G / 4)]
        bbase = bases[:, BBASE:ALL_BASES]
        node_at = sb("node_at", [P, NB])
        sel = sb("sel", [P, COLS])
        spare = gring[:].rearrange("p s t f -> p (s t f)")
        assert len(regions) * (COLS + 32) <= GSLOT * T * D
        unit_bases = [spare[0:r.blocks, len(regions) * COLS + i * 32:len(regions) * COLS + i * 32 + r.padded] for i, r in enumerate(regions)]
        nodes = [spare[0:r.blocks, i * COLS:(i + 1) * COLS] for i, r in enumerate(regions)]
        base_f = sb("base_f", [P, S])
        tile_lo = sb("tile_lo", [P, TR])
        tile_hi = sb("tile_hi", [P, TR])
        tile_base = sb("tile_base", [P, TR])
        flag_f = sb("flag_f", [1, 4])
        flag_b = sb("flag_b", [P, 4])
        flag = sb("flag", [1, 1], I32)
        w0 = sb("w0", [P, HID])
        w1 = sb("w1", [HID, HID])
        w2 = sb("w2", [HID, D])
        wc = sb("wc", [P, 3, D])
        bias = sb("bias", [HID, 4])
        brow = sb("brow", [P, 4, D])
        eps = sb("eps", [P, 1])
        stat = sb("stat", [P, 3, NR])
        degs = sb("degs", [P, NR])
        dinv = sb("dinv", [D, 2, CH])
        prod = sb("prod", [P, 3 * D])
        psum = ctx.enter_context(nc.psum_tensor("psum", [P, 8, 512], F32))
        ps = [psum[:, i, :] for i in range(8)]
        PROD, TURN, WBANK = 4, 5, 6

        tile_dram = nc.dram_tensor("tile_dram", [3, NT], F32).ap()
        base_dram = nc.dram_tensor("base_dram", [ALL_BASES], I32).ap()
        deg_dram = nc.dram_tensor("deg_dram", [N], F32).ap()
        dinv_dram = nc.dram_tensor("dinv_dram", [N], F32).ap()
        resid_dram = nc.dram_tensor("resid_dram", [CP, NRD], F32).ap()
        tables = [nc.dram_tensor(f"h_table{i}", [N, D], F32).ap() for i in range(3)]
        x1_dram = nc.dram_tensor("x1_dram", [N, D], F32).ap()
        count_dram = nc.dram_tensor("count_dram", [NB, CP, 2 * CB], BF16).ap()

        s_go = sem("s_go")
        s_w = sem("s_w")
        s_x = sem("s_x")
        s_dst = sem("s_dst")
        s_src = sem("s_src")
        s_const = sem("s_const")
        s_tiles = sem("s_tiles")
        s_tiles_st = sem("s_tiles_st")
        s_tiles_ld = sem("s_tiles_ld")
        s_tbase = sem("s_tbase")
        s_tbase_st = sem("s_tbase_st")
        s_tbase_ld = sem("s_tbase_ld")
        s_bases = sem("s_bases")
        s_bases_st = sem("s_bases_st")
        s_bases_ld = sem("s_bases_ld")
        s_ub = sem("s_ub")
        s_nodes = sem("s_nodes")
        s_nodes_t = sem("s_nodes_t")
        s_node_at = sem("s_node_at")
        s_sel = sem("s_sel")
        s_flag_w = sem("s_flag_w")
        s_flag_b = sem("s_flag_b")
        s_flag = sem("s_flag")
        s_row = sem("s_row")
        s_turn = sem("s_turn")
        s_turned = sem("s_turned")
        s_dv = sem("s_dv")
        s_sq_in = sem("s_sq_in")
        s_sq = sem("s_sq")
        s_var = sem("s_var")
        s_root = sem("s_root")
        s_h = sem("s_h")
        s_ht = sem("s_ht")
        s_hc = sem("s_hc")
        s_resid = sem("s_resid")
        s_resid_st = sem("s_resid_st")
        s_resid_ld = sem("s_resid_ld")
        s_attr = [sem(f"s_attr{i}") for i in range(RING)]
        s_oh = sem("s_oh")
        s_mm = sem("s_mm")
        s_add0 = sem("s_add0")
        s_deg = sem("s_deg")
        s_deg_all = sem("s_deg_all")
        s_deg_st = sem("s_deg_st")
        s_deg_ld = sem("s_deg_ld")
        s_dinv = sem("s_dinv")
        s_dinv_st = sem("s_dinv_st")
        s_pass = sem("s_pass")
        s_m1 = sem("s_m1")
        s_a1 = sem("s_a1")
        s_m2 = sem("s_m2")
        s_a2 = sem("s_a2")
        s_m3 = sem("s_m3")
        s_y = sem("s_y")
        s_x1 = sem("s_x1")
        s_x1_st = sem("s_x1_st")
        s_tab = sem("s_tab")
        s_hi = sem("s_hi")
        s_t = sem("s_t")
        s_mid = sem("s_mid")
        s_parts = sem("s_parts")
        s_zero = sem("s_zero")
        s_idx = sem("s_idx")
        s_rows = [sem(f"s_rows{i}") for i in range(GSLOT)]
        s_goh = sem("s_goh")
        s_win = sem("s_win")
        s_add = sem("s_add")
        s_unit = sem("s_unit")
        s_built = sem("s_built")
        s_banks = sem("s_banks")
        s_stored = sem("s_stored")
        s_count_st = sem("s_count_st")
        s_count_ld = [sem("s_count_ld0"), sem("s_count_ld1")]
        s_mul = sem("s_mul")
        s_prod = sem("s_prod")
        s_tr = sem("s_tr")
        s_dadd = sem("s_dadd")
        s_scaled = sem("s_scaled")
        s_dchunk = [sem("s_dchunk0"), sem("s_dchunk1")]
        s_conv = sem("s_conv")
        s_act = sem("s_act")
        s_tp = sem("s_tp")
        s_stage = sem("s_stage")
        s_store = [sem("s_store0"), sem("s_store1")]
        s_res = [sem("s_res0"), sem("s_res1")]
        s_o = sem("s_o")
        w_row = sem("w_row")
        w_rows = sem("w_rows")
        w_idx = sem("w_idx")
        w_oh = sem("w_oh")
        w_mm = sem("w_mm")
        w_add = sem("w_add")
        w_iota = sem("w_iota")
        w_deg = sem("w_deg")

        cidx = lambda k: slice(k * CH, (k + 1) * CH)
        N_W = 18

        def column(rows, k, j):
            return agg_h[rows, k * CH + j:(k + 1) * CH:J]

        def table_chunk(t, k):
            return t[k * CH:(k + 1) * CH, :].rearrange("(p j) f -> p (j f)", j=J)

        attr_v = edge_attr.rearrange("(g p t) f -> g p (t f)", p=P, t=T)
        tile_of = ring.rearrange("p s (t f) -> p s t f", f=D)
        drow, arow, prow = (agg_h[0:Q, i * RE:(i + 1) * RE] for i in range(3))
        raw, rawf, rel_row = (big[0:Q, 2 * NRD + i * RE:2 * NRD + (i + 1) * RE] for i in range(3))
        by_tile = lambda a: a.rearrange("q (c e) -> q c e", e=P)
        lo_row, hi_row = key[0:1, :], who[0:1, :]
        row_work = big[0:1, 0:2 * (NU + G + NG + NB)]
        sq = agg_h[0:CP, 0:NRD]
        rows3 = lambda a: a.rearrange("p (r f) -> p r f", f=D)
        wide = lambda a: a.unsqueeze(2).to_broadcast([CP, NR, D])
        feat = lambda i: brow[0:CP, i:i + 1, :].to_broadcast([CP, NR, D])
        table_v = lambda c: c.rearrange("p (q c) -> p q c", c=TR)
        turns = [(rel_row, "strided", table_v(rel0)),
                 (arow, "dense", table_v(key[:])), (drow, "gathered", table_v(key[:])),
                 (prow, "dense", table_v(who[:])), (rawf, "gathered", table_v(who[:]))]

        def rows_of(kind, c):
            edge = min(Q, max(0, ceil((TD - c) / TR)))
            return {"strided": (0, Q), "dense": (0, edge), "gathered": (edge, Q)}[kind]

        pieces = [(n, c) for n, (_, kind, _) in enumerate(turns) for c in range(TR)
                  if rows_of(kind, c)[0] < rows_of(kind, c)[1]]

        def stored(eng, n):
            if n >= 2:
                eng.wait_ge(s_store[n % 2], 16 * (n // 2))

        def load_attr(sp, s, group, landed):
            sp.dma_start(ring[:, s, :], attr_v[bass.ds(group, 1)].rearrange("o p r -> (o p) r")).then_inc(landed, 16)

        def store_out(sp, k):
            n = 2 * NC + k
            sp.wait_ge(s_o, k + 1)
            sp.dma_start(table_chunk(out, k), stage[0:CP, n % 2, :]).then_inc(s_store[n % 2], 16)

        def load_dinv(sp, n):
            if n >= 2:
                sp.wait_ge(s_scaled, n - 1)
            k = n % NC
            sp.dma_start(dinv[:, n % 2, :], dinv_dram[cidx(k)].rearrange("(o c) -> o c", o=1).to_broadcast([D, CH])
                         ).then_inc(s_dchunk[n % 2], 16)

        def copy_h(act, n):
            for k in range(NC):
                act.wait_ge(s_ht, n * NC + k + 1)
                nc.scalar.copy(agg_h[D:2 * D, cidx(k)].rearrange("f (p j) -> f j p", j=J),
                               ps[4 + k % 2][0:D, 0:CH].rearrange("f (j p) -> f j p", j=J)).then_inc(s_hc, 1)

        def transpose_h(pe, n):
            pe.wait_ge(s_h, n + 1)
            for k in range(NC):
                if k >= 2:
                    pe.wait_ge(s_hc, n * NC + k - 1)
                for j in range(J):
                    r = k * J + j
                    mm = nc.tensor.transpose(ps[4 + k % 2][0:D, j * CP:(j + 1) * CP], hrows[:, r * D:(r + 1) * D],
                                             ident[0:CP, 0:CP])
                mm.then_inc(s_ht, 1)

        def after_conv(dve, layer, k, output_rows, own):
            if layer == 2:
                output_rows(k)
            else:
                dve.wait_ge(s_conv, layer * NC + k + 1)
                own(nc.vector.memset(agg_h[0:D, cidx(k)], 0.0))

        def walk(eng, layer, step, group):
            for r in regions:
                if layer == 0:
                    step(r, 0, None, 0)
                    if r.pairs > 1:
                        with eng.Fori(0, r.pairs - 1) as i:
                            step(r, 2 * i + 1, 2 * i, 1)
                            step(r, 2 * i + 2, 2 * i + 1, 0)
                    step(r, r.blocks - 1, r.blocks - 2, 1)
                    step(r, None, r.blocks - 1, 0)
                else:
                    with eng.Fori(0, r.pairs) as i:
                        step(r, 2 * i, 2 * i, 0)
                        step(r, 2 * i + 1, 2 * i + 1, 1)
            if REST4:
                with eng.Fori(0, REST4) as i:
                    for s in range(4):
                        group(PAIRED + s + 4 * i, s)
            for g in range(REST, G):
                group(g, g % GSLOT)

        block = ctx.enter_context(nc.Block())

        @block.sync
        def _(sp):
            sp.dma_start(raw.bitcast(I32), dst.rearrange("(q n) -> q n", q=Q)).then_inc(s_dst, 16)
            sp.dma_start(rawf.bitcast(I32), src.rearrange("(q n) -> q n", q=Q)).then_inc(s_src, 16)
            sp.dma_start(xrows.rearrange("p (k r) -> p k r", k=NC),
                         x.rearrange("(k p j) f -> p k (j f)", p=CP, j=J)).then_inc(s_x, 16)
            sp.dma_start(w0[0:D, :], W0[D:2 * D, :]).then_inc(s_w, 16)
            sp.dma_start(w0[D:2 * D, :], W0[0:D, :]).then_inc(s_w, 16)
            sp.dma_start(w1[:], W1).then_inc(s_w, 16)
            sp.dma_start(w2[:], W2).then_inc(s_w, 16)
            for i, (wl, wr) in enumerate(((W1l, W1r), (W2l, W2r), (W3l, W3r))):
                sp.dma_start(wc[0:D, i, :], wl).then_inc(s_w, 16)
                sp.dma_start(wc[D:2 * D, i, :], wr).then_inc(s_w, 16)
            for i, b in enumerate((b0, b1, c1, c2)):
                sp.dma_start(bias[0:b.shape[0], i:i + 1], b.rearrange("(p o) -> p o", o=1)).then_inc(s_w, 16)
            for i, b in enumerate((b2, ln_g, ln_b, c3)):
                sp.dma_start(brow[:, i, :], b.rearrange("(o f) -> o f", o=1).to_broadcast([P, D])).then_inc(s_w, 16)
            sp.wait_ge(s_tiles, 2)
            for i, a in enumerate((tile_lo, tile_hi)):
                sp.dma_start(tile_dram[i].rearrange("(q c) -> q c", q=Q), a[0:Q, :]).then_inc(s_tiles_st, 16)
            sp.wait_ge(s_tiles_st, 32)
            for i, a in enumerate((lo_row, hi_row)):
                sp.dma_start(a, tile_dram[i:i + 1, :]).then_inc(s_tiles_ld, 16)
            sp.wait_ge(s_tbase, 1)
            sp.dma_start(tile_dram[2:3, :], hi_row).then_inc(s_tbase_st, 16)
            sp.wait_ge(s_tbase_st, 16)
            sp.dma_start(tile_base[0:Q, :], tile_dram[2].rearrange("(q c) -> q c", q=Q)).then_inc(s_tbase_ld, 16)
            sp.wait_ge(s_bases, 1)
            sp.dma_start(base_dram.rearrange("(o n) -> o n", o=1), bases[:, 0:ALL_BASES]).then_inc(s_bases_st, 16)
            sp.wait_ge(s_bases_st, 16)
            for r, to in zip(regions, unit_bases):
                sp.dma_start(to.bitcast(I32), base_dram[r.first_base:r.first_base + r.blocks * r.padded]
                             .rearrange("(b u) -> b u", u=r.padded)).then_inc(s_ub, 16)
            sp.wait_ge(s_resid, 2)
            sp.dma_start(resid_dram, xrows).then_inc(s_resid_st, 16)

            sp.wait_ge(s_turned, len(pieces))
            sp.wait_ge(s_flag, 1)
            covered = sp.value_load(flag[0:1, 0:1], min_val=0, max_val=1)
            with sp.If(covered == 1):
                for s in range(RING):
                    load_attr(sp, s, s, s_attr[s])
                with sp.Fori(0, NIT - 1) as i:
                    for m in range(BODY):
                        sp.wait_ge(s_mm, i * BODY + (m + 1))
                        load_attr(sp, m % RING, i * BODY + (m + RING), s_attr[m % RING])
                for m in range(NG - BODY, NG - RING):
                    sp.wait_ge(s_mm, m + 1)
                    load_attr(sp, m % RING, m + RING, s_attr[m % RING])
            with sp.Else():
                with sp.Fori(0, NG) as g:
                    sp.wait_ge(w_add, g * NWIN + 1)
                    load_attr(sp, 0, g, w_row)

            sp.wait_ge(s_pass, 1)
            sp.dma_start(deg_dram.rearrange("(o n) -> o n", o=1), deg[:, 0:N]).then_inc(s_deg_st, 16)
            sp.wait_ge(s_bases_st, 16)
            sp.dma_start(bases[:, 0:ALL_BASES], base_dram.rearrange("(o n) -> o n", o=1)).then_inc(s_bases_ld, 16)
            sp.wait_ge(s_deg_st, 16)
            sp.dma_start(degs[0:CP, :], deg_dram.rearrange("(p c) -> p c", p=CP)).then_inc(s_deg_ld, 16)
            sp.wait_ge(s_resid_st, 16)
            sp.dma_start(xrows, resid_dram).then_inc(s_resid_ld, 16)
            sp.wait_ge(s_dinv, 1)
            sp.dma_start(dinv_dram.rearrange("(p c) -> p c", p=CP), degs[0:CP, :]).then_inc(s_dinv_st, 16)

            sp.wait_ge(s_x1, 1)
            sp.dma_start(x1_dram.rearrange("(k p j) f -> p k (j f)", p=CP, j=J),
                         yrows.rearrange("p (k r) -> p k r", k=NC)).then_inc(s_x1_st, 16)
            sp.wait_ge(s_h, 2)
            sp.dma_start(tables[0].rearrange("(k p j) f -> p k (j f)", p=CP, j=J),
                         hrows.rearrange("p (k r) -> p k r", k=NC)).then_inc(s_tab, 16)
            sp.wait_ge(s_dinv_st, 16)
            sp.sem_inc(s_stored, 2)
            for layer in range(3):
                for n in range(2):
                    load_dinv(sp, layer * NC + n)

                def count_step(r, built, multiplied, c):
                    if layer == 0:
                        if built is None:
                            return
                        b = built + r.first_block
                        sp.wait_ge(s_banks, (built + 1) * (r.units * len(r.quanta)) + (r.first_quantum + 2))
                        sp.dma_start(count_dram[bass.ds(b, 1)].rearrange("o p n -> (o p) n"),
                                     counts[c].rearrange("p d a -> p (d a)")).then_inc(s_count_st, 16)
                        sp.wait_ge(s_count_st, (b + 1) * 16)
                        sp.sem_inc(s_stored, 1)
                    else:
                        b = multiplied + r.first_block
                        sp.wait_ge(s_mul, b + (layer * NB + 1))
                        sp.dma_start(counts[c].rearrange("p d a -> p (d a)"),
                                     count_dram[bass.ds(b, 1)].rearrange("o p n -> (o p) n")).then_inc(s_count_ld[c], 16)

                with sp.If(covered == 1):
                    walk(sp, layer, count_step, lambda g, s: None)
                with sp.Else():
                    sp.sem_inc(s_go, 1)
                if layer == 2:
                    break
                for k in range(NC):
                    n = layer * NC + k
                    sp.wait_ge(s_stage, n + 1)
                    sp.dma_start(table_chunk(tables[layer + 1], k), stage[0:CP, n % 2, :]).then_inc(s_store[n % 2], 16)
                    if k + 2 < NC:
                        load_dinv(sp, n + 2)
            sp.wait_ge(s_x1_st, 16)
            for k in range(NC):
                if k >= 2:
                    sp.wait_ge(s_o, k - 1)
                sp.dma_start(resid[0:CP, k % 2, :], table_chunk(x1_dram, k)).then_inc(s_res[k % 2], 16)
                if k >= 1:
                    store_out(sp, k - 1)
                if k + 2 < NC:
                    load_dinv(sp, 2 * NC + k + 2)
            store_out(sp, NC - 1)
            for b in range(2):
                sp.wait_ge(s_store[b], 16 * len([n for n in range(3 * NC) if n % 2 == b]))

        @block.gpsimd
        def _(pool):
            nc.gpsimd.memset(ident[:], 0.0).then_inc(s_const, 1)
            nc.gpsimd.iota(iota[:], pattern=[[1, WIN]], base=0, channel_multiplier=0,
                           allow_small_or_imprecise_dtypes=True).then_inc(s_const, 1)
            nc.gpsimd.iota(iota16[:], pattern=[[1, max(P, WMAX * NR)]], base=0, channel_multiplier=0,
                           allow_small_or_imprecise_dtypes=True).then_inc(s_const, 1)
            nc.gpsimd.memset(ones[:], 1.0).then_inc(s_const, 1)
            nc.gpsimd.memset(ones16[:], 1.0).then_inc(s_const, 1)
            nc.gpsimd.memset(eps[:], EPS).then_inc(s_const, 1)
            pool.wait_ge(s_const, 6)
            nc.gpsimd.affine_select(out=ident[:], in_=ident[:], compare_op=ALU.not_equal, fill=1.0, base=0,
                                    pattern=[[-1, P]], channel_multiplier=1).then_inc(s_const, 1)
            pool.wait_ge(s_h, 1)
            pool.wait_ge(s_w, 16 * N_W)
            nc.gpsimd.tensor_tensor(xrows, xrows, hrows, ALU.add).then_inc(s_resid, 1)
            pool.wait_ge(s_resid, 1)
            nc.gpsimd.tensor_tensor(rows3(xrows), rows3(xrows), feat(2), ALU.add).then_inc(s_resid, 1)
            pool.wait_ge(s_sq_in, 3)
            nc.gpsimd.tensor_tensor(rows3(yrows), rows3(yrows), feat(3), ALU.add).then_inc(s_x1, 1)
            pool.wait_ge(s_flag, 1)
            covered = pool.value_load(flag[0:1, 0:1], min_val=0, max_val=1)
            for layer in range(3):
                if layer == 0:
                    pool.wait_ge(s_tab, 16)
                else:
                    for b in range(2):
                        pool.wait_ge(s_store[b], 16 * len([n for n in range(layer * NC) if n % 2 == b]))
                table = tables[layer]

                def gather(slot, c, landed):
                    nc.gpsimd.indirect_dma_start(
                        out=gring[:, slot, c, :], out_offset=None, in_=table,
                        in_offset=bass.IndirectOffsetOnAxis(ap=idx[:, slot, c:c + 1], axis=0)).then_inc(landed, 16)

                def gather_group(g, s):
                    pool.wait_ge(s_idx, g + (layer * G + 1))
                    pool.wait_ge(s_win, g + (layer * G + 1))
                    pool.sem_inc(s_go, 1)
                    for c in range(T):
                        gather(s, c, s_rows[s])

                with pool.If(covered == 1):
                    with pool.Fori(0, REST // 4) as i:
                        for s in range(GSLOT):
                            gather_group(i * 4 + s, s)
                    for g in range(REST, G):
                        gather_group(g, g % GSLOT)
                with pool.Else():
                    with pool.Fori(0, NG) as g:
                        pool.wait_ge(w_idx, g + (layer * NG + 1))
                        pool.wait_ge(w_add, (g + (layer + 1) * NG) * NWIN + 1)
                        pool.sem_inc(s_go, 1)
                        for c in range(T):
                            gather(0, c, w_rows)
                if layer == 2:
                    break
                for k in range(NC):
                    n = layer * NC + k
                    rows = parts[:, k * J:(k + 1) * J, :, :]
                    left = pool_left[0:CP, :].rearrange("p (j f) -> p j f", f=D)
                    pool.wait_ge(s_stage, n + 1)
                    pool.wait_ge(s_hi, 1 + n + 1)
                    nc.gpsimd.tensor_tensor(left, stage[0:CP, n % 2, :].rearrange("p (j f) -> p j f", f=D), rows[:, :, 0, :],
                                            ALU.subtract).then_inc(s_t, 1)
                    pool.wait_ge(s_t, 1 + n + 1)
                    nc.gpsimd.tensor_copy(rows[:, :, 1, :], left).then_inc(s_mid, 1)
                    pool.wait_ge(s_mid, 1 + n + 1)
                    nc.gpsimd.tensor_tensor(rows[:, :, 2, :], left, rows[:, :, 1, :], ALU.subtract).then_inc(s_parts, 1)
                    pool.wait_ge(s_parts, 1 + n + 1)

        @block.scalar
        def _(act):
            def layernorm_roots(n):
                act.wait_ge(s_sq_in, n + 1)
                nc.scalar.activation(sq, hrows if n != 1 else yrows, ACT.Square).then_inc(s_sq, 1)
                act.wait_ge(s_var, n + 1)
                nc.scalar.activation(stat[0:CP, 2, :], stat[0:CP, 1, :], ACT.Sqrt, bias=eps[0:CP, :],
                                     scale=1.0 / D).then_inc(s_root, 1)

            act.wait_ge(s_const, 7)
            act.sem_inc(s_banks, 2)
            act.sem_inc(s_prod, 1)
            for m, (n, c) in enumerate(pieces):
                _, kind, to = turns[n]
                a, b = rows_of(kind, c)
                act.wait_ge(s_turn, m + 1)
                nc.scalar.copy(to[:, a:b, c], ps[m % 4][:, a:b]).then_inc(s_turned, 1)
            layernorm_roots(0)
            copy_h(act, 0)
            act.wait_ge(s_flag, 1)
            covered = act.value_load(flag[0:1, 0:1], min_val=0, max_val=1)
            act.wait_ge(s_w, 16 * N_W)
            for step in range(NC + 1):
                if step < NC:
                    k = step
                    act.wait_ge(s_m1, k + 1)
                    if k >= 2:
                        act.wait_ge(s_m2, k - 1)
                    nc.scalar.activation(hid_v[:, 0, k % 2, :], ps[k % 2][:, 0:CH], ACT.Relu, bias=bias[:, 0:1]).then_inc(s_a1, 1)
                if step >= 1:
                    k = step - 1
                    act.wait_ge(s_m2, k + 1)
                    if k >= 2:
                        act.wait_ge(s_m3, k - 1)
                    nc.scalar.activation(hid_v[:, 1, k % 2, :], ps[2 + k % 2][:, 0:CH], ACT.Relu, bias=bias[:, 1:2]).then_inc(s_a2, 1)
            layernorm_roots(1)
            layernorm_roots(2)
            act.wait_ge(s_nodes_t, 1)
            nc.scalar.copy(node_at[:], ps[WBANK][:, 0:NB]).then_inc(s_node_at, 1)
            copy_h(act, 1)
            act.wait_ge(s_x1_st, 16)
            nc.scalar.copy(parts[:, :, 0, :], rows3(hrows)).then_inc(s_hi, 1)
            act.wait_ge(s_t, 1)
            nc.scalar.copy(parts[:, :, 1, :], rows3(xrows)).then_inc(s_mid, 1)
            act.wait_ge(s_zero, 1)
            for layer in range(3):
                def copy_idx(g, s):
                    act.wait_ge(s_win, g + (layer * G + 1))
                    nc.scalar.copy(idx[:, s, :], who[:, bass.ds(g * T + TD, T)]).then_inc(s_idx, 1)

                def copy_quantum(r, b, u, q, c):
                    n = r.quanta[q]
                    col = u * r.w + 2 * sum(r.quanta[:q])
                    nq = len(r.quanta)
                    at = b * (r.units * nq) + (r.first_quantum + u * nq + q)
                    pair = ((u + c * r.units) * nq + q) % 2
                    act.wait_ge(s_built, at + 3)
                    if u == 0 and q == 0:
                        act.wait_ge(s_mul, b + (r.first_block + 1))
                        act.wait_ge(s_stored, b + (r.first_block + 1))
                    nc.scalar.copy(counts[c][:, col:col + 2 * n, :].rearrange("p (h d) a -> p h (d a)", h=2),
                                   psum[0:CP, 2 * pair:2 * pair + 2, 0:n * NR]).then_inc(s_banks, 1)

                def copy_product(b):
                    act.wait_ge(s_mul, b + (layer * NB + 3))
                    act.wait_ge(s_tr, b + (layer * NB + 1))
                    nc.scalar.copy(prod[:], ps[PROD][:, 0:3 * D]).then_inc(s_prod, 1)

                def step(r, built, multiplied, c):
                    b = built if built is not None else multiplied
                    if built is not None:
                        for s in range(3, 5):
                            copy_idx((built + r.first_block) * 2 + s, (2 * c + s) % GSLOT)
                    for u in range(r.units if layer == 0 and built is not None else 0):
                        for q in range(len(r.quanta)):
                            copy_quantum(r, built, u, q, c)
                        if u == r.units - 3 and multiplied is not None:
                            copy_product(multiplied + r.first_block)
                    if multiplied is not None and (layer > 0 or built is None):
                        copy_product(multiplied + r.first_block)

                with act.If(covered == 1):
                    for s in range(3):
                        copy_idx(s, s)
                    walk(act, layer, step, lambda g, s: copy_idx(g + 3, (s + 3) % GSLOT) if not isinstance(g, int) or g + 3 < G else None)
                with act.Else():
                    with act.Fori(0, NG) as g:
                        act.wait_ge(w_add, (g + (layer + 1) * NG) * NWIN + 1)
                        nc.scalar.copy(idx[:, 0, :], who[:, bass.ds(g * T, T)]).then_inc(w_idx, 1)
                if layer == 2:
                    break
                for k in range(NC):
                    n = layer * NC + k
                    act.wait_ge(s_conv, n + 1)
                    nc.scalar.activation(agg_h[D:2 * D, cidx(k)], ps[k % 2][0:D, 0:CH], ACT.Relu,
                                         bias=bias[0:D, 2 + layer:3 + layer]).then_inc(s_act, 1)
                    act.wait_ge(s_tp, n + 1)
                    stored(act, n)
                    if n >= 2:
                        act.wait_ge(s_parts, 1 + n - 1)
                    nc.scalar.copy(stage[0:CP, n % 2, :], ps[2 + k % 2][0:CP, 0:J * D]).then_inc(s_stage, 1)
                    nc.scalar.copy(parts[:, k * J:(k + 1) * J, 0, :],
                                   ps[2 + k % 2][0:CP, 0:J * D].rearrange("p (j f) -> p j f", f=D)).then_inc(s_hi, 1)

        @block.tensor
        def _(pe):
            pe.wait_ge(s_const, 7)
            pe.sem_inc(s_win, GSLOT)
            pe.sem_inc(s_built, 2)
            pe.sem_inc(s_mul, 2)
            pe.sem_inc(s_tr, 1)
            pe.wait_ge(s_flag_w, 1)
            nc.tensor.matmul(ps[7][:, 0:3], ones[0:1, :], flag_f[0:1, 1:4], start=True, stop=True).then_inc(s_flag_b, 1)
            for m, (n, c) in enumerate(pieces):
                row, kind, _ = turns[n]
                if m == 0 or pieces[m - 1][0] != n:
                    pe.wait_ge(s_row, n + 1)
                if m >= 4:
                    pe.wait_ge(s_turned, m - 3)
                cols = row[:, (c // T) * GE + c % T:(c // T + 1) * GE:T] if kind == "strided" else row[:, c * P:(c + 1) * P]
                nc.tensor.transpose(ps[m % 4][:, 0:Q], cols, ident[0:Q, 0:Q]).then_inc(s_turn, 1)
            transpose_h(pe, 0)
            pe.wait_ge(s_flag, 1)
            covered = pe.value_load(flag[0:1, 0:1], min_val=0, max_val=1)

            def window(tiles, oh, bank, done, with_deg=False):
                for t in range(T):
                    mm = nc.tensor.matmul(ps[bank][0:D, 0:WIN], tiles[:, t, :], onehot[:, oh, t, :],
                                          start=(t == 0), stop=(t == T - 1))
                if with_deg:
                    for t in range(T):
                        mm = nc.tensor.matmul(ps[bank][0:1, WIN:2 * WIN], ones16[:],
                                              onehot[:, oh, t, :].bitcast(BF16)[:, 1:2 * WIN:2],
                                              start=(t == 0), stop=(t == T - 1))
                mm.then_inc(done, 1)

            pe.wait_ge(s_turned, len(pieces))
            pe.wait_ge(s_hc, NC)
            with pe.If(covered == 1):
                with pe.Fori(0, NIT) as i:
                    for m in range(BODY):
                        pe.wait_ge(s_attr[m % RING], i * (16 * BODY // RING) + 16 * (m // RING + 1))
                        pe.wait_ge(s_oh, i * BODY + (m + 1))
                        window(tile_of[:, m % RING], m % OH_SLOTS, m % 5, s_mm, True)
            with pe.Else():
                with pe.Fori(0, NG) as g:
                    with pe.Fori(0, NWIN) as k:
                        pe.wait_ge(w_row, (g + 1) * 16)
                        pe.wait_ge(w_oh, g * NWIN + k + 1)
                        window(tile_of[:, 0], 0, 0, w_mm, True)
            pe.wait_ge(s_pass, 1)
            pe.wait_ge(s_w, 16 * N_W)
            for step in range(NC + 2):
                if step < NC:
                    k = step
                    if k >= 2:
                        pe.wait_ge(s_a1, k - 1)
                    nc.tensor.matmul(ps[k % 2][:, 0:CH], w0[:], agg_h[:, cidx(k)], start=True, stop=True).then_inc(s_m1, 1)
                if 1 <= step <= NC:
                    k = step - 1
                    pe.wait_ge(s_a1, k + 1)
                    if k >= 2:
                        pe.wait_ge(s_a2, k - 1)
                    nc.tensor.matmul(ps[2 + k % 2][:, 0:CH], w1[:], hid_v[:, 0, k % 2, :], start=True, stop=True).then_inc(s_m2, 1)
                if step >= 2:
                    k = step - 2
                    pe.wait_ge(s_a2, k + 1)
                    if k >= 2:
                        pe.wait_ge(s_y, k - 1)
                    for j in range(J):
                        mm = nc.tensor.matmul(ps[4 + k % 2][0:CP, j * D:(j + 1) * D], hid_v[:, 1, k % 2, j:CH:J], w2[:],
                                              start=True, stop=True)
                    mm.then_inc(s_m3, 1)
            pe.wait_ge(s_nodes, 1)
            for r, rows in zip(regions, nodes):
                mm = nc.tensor.transpose(ps[WBANK][:, r.first_block:r.first_block + r.blocks], rows, ident[0:r.blocks, 0:r.blocks])
            mm.then_inc(s_nodes_t, 1)
            transpose_h(pe, 1)
            pe.wait_ge(s_hc, 2 * NC)
            for layer in range(3):
                def gathered(g, s):
                    pe.wait_ge(s_rows[s], g * (4 * T) + ((1 + layer * slot_uses[s]) * 16 * T - s * 4 * T))
                    pe.wait_ge(s_goh, g + (layer * G + 1))
                    pe.wait_ge(s_add, g + (layer * G + 1))
                    window(gring[:, s], s, WBANK + s % 2, s_win)

                def build(r, b, u, c):
                    nq = len(r.quanta)
                    pe.wait_ge(s_unit, b * r.units + (r.first_unit + u + 1))
                    for q, n in enumerate(r.quanta):
                        pair = ((u + c * r.units) * nq + q) % 2
                        pe.wait_ge(s_banks, b * (r.units * nq) + (r.first_quantum + u * nq + q + 1))
                        for half in range(2):
                            col = (2 * sum(r.quanta[:q]) + half * n) * NR
                            oh = unit_oh[(u + c * r.units) % 2]
                            for t in range(r.k):
                                mm = nc.tensor.matmul(psum[0:CP, 2 * pair + half, 0:n * NR],
                                                      oh[:, KW * NR + t * P:KW * NR + t * P + CP],
                                                      oh[:, t * r.w * NR + col:t * r.w * NR + col + n * NR],
                                                      start=(t == 0), stop=(t == r.k - 1))
                        mm.then_inc(s_built, 1)

                def multiply(b, c, first, end):
                    if first == 0:
                        pe.wait_ge(s_prod, b + (layer * NB + 1))
                    for a in range(first, end):
                        mm = nc.tensor.matmul(ps[PROD][:, 0:3 * D], counts[c][:, :, a],
                                              parts[:, a, :, :].rearrange("p s f -> p (s f)"),
                                              start=(a == 0), stop=(a == NR - 1))
                    if end == NR:
                        mm.then_inc(s_mul, 1)

                def turn(r, b):
                    at = b + (layer * NB + r.first_block)
                    pe.wait_ge(s_prod, at + 2)
                    pe.wait_ge(s_dadd, b + (layer * NB + r.first_block + 1))
                    pe.wait_ge(s_sel, b + (layer * NB + r.first_block + 1))
                    for i in range(3):
                        mm = nc.tensor.matmul(ps[TURN][0:D, 0:COLS], prod[:, (2 - i) * D:(3 - i) * D], sel[:],
                                              start=(i == 0), stop=(i == 2))
                    mm.then_inc(s_tr, 1)

                def step(r, built, multiplied, c):
                    pair = None
                    if built is not None:
                        g = (built + r.first_block) * 2
                        s = 2 * c
                        gathered(g, s)
                    if layer == 0 and built is not None:
                        if multiplied is not None:
                            pe.wait_ge(s_banks, (multiplied + 1) * (r.units * len(r.quanta)) + (r.first_quantum + 2))
                        spread = [NR * u // (r.units - 2) for u in range(r.units - 1)]
                        for u in range(r.units):
                            build(r, built, u, c)
                            if u <= r.units - 3 and multiplied is not None:
                                multiply(multiplied + r.first_block, 1 - c, spread[u], spread[u + 1])
                            if u == r.units // 2:
                                gathered(g + 1, s + 1)
                            if u == r.units - 2 and multiplied is not None:
                                turn(r, multiplied)
                    elif layer == 0:
                        pe.wait_ge(s_banks, (multiplied + 1) * (r.units * len(r.quanta)) + (r.first_quantum + 2))
                        multiply(multiplied + r.first_block, 1 - c, 0, NR)
                        turn(r, multiplied)
                    else:
                        pe.wait_ge(s_count_ld[c], multiplied * 8 + ((r.first_block // 2 + 1 + (layer - 1) * (NB // 2)) * 16 - 8 * c))
                        multiply(multiplied + r.first_block, c, 0, NR)
                        gathered(g + 1, s + 1)
                        turn(r, multiplied)

                if layer == 0:
                    pe.wait_ge(s_parts, 1)
                    pe.wait_ge(s_node_at, 1)
                with pe.If(covered == 1):
                    walk(pe, layer, step, gathered)
                with pe.Else():
                    with pe.Fori(0, NG) as g:
                        with pe.Fori(0, NWIN) as k:
                            pe.wait_ge(w_rows, (g + (1 + layer * NG)) * (16 * T))
                            pe.wait_ge(w_oh, (g + (layer + 1) * NG) * NWIN + k + 1)
                            window(gring[:, 0], 0, 0, w_mm)
                if layer == 2:
                    break

                def to_rows(k):
                    n = layer * NC + k
                    pe.wait_ge(s_act, n + 1)
                    if n >= 2:
                        pe.wait_ge(s_hi, 1 + n - 1)
                    for j in range(J):
                        mm = nc.tensor.transpose(ps[2 + k % 2][0:CP, j * D:(j + 1) * D], column(slice(D, 2 * D), k, j),
                                                 ident[D:2 * D, D:2 * D])
                    mm.then_inc(s_tp, 1)

                for k in range(NC):
                    n = layer * NC + k
                    pe.wait_ge(s_scaled, n + 1)
                    if n >= 2:
                        pe.wait_ge(s_act, n - 1)
                    nc.tensor.matmul(ps[k % 2][0:D, 0:CH], wc[:, layer, :], agg_h[:, cidx(k)], start=True, stop=True).then_inc(s_conv, 1)
                    if k >= 1:
                        to_rows(k - 1)
                to_rows(NC - 1)
                pe.wait_ge(s_hi, 1 + (layer + 1) * NC)
                pe.wait_ge(s_parts, 1 + (layer + 1) * NC)
            for k in range(NC):
                pe.wait_ge(s_scaled, 2 * NC + k + 1)
                if k >= 2:
                    pe.wait_ge(s_o, k - 1)
                for j in range(J):
                    mm = nc.tensor.matmul(ps[k % 2][0:CP, j * D:(j + 1) * D], column(slice(0, P), k, j), wc[:, 2, :],
                                          start=True, stop=True)
                mm.then_inc(s_conv, 1)

        @block.vector
        def _(dve):
            steps = [0]

            def own(ins):
                steps[0] += 1
                ins.then_inc(s_dv, 1)
                dve.wait_ge(s_dv, steps[0])

            v = nc.vector
            ts = v.tensor_scalar
            dve.wait_ge(s_dst, 16)
            own(v.memset(bases[:], 0))
            own(v.tensor_copy(drow, raw.bitcast(I32)))
            v.tensor_reduce(tile_lo[0:Q, :], by_tile(drow), AX, ALU.min).then_inc(s_tiles, 1)
            v.tensor_reduce(tile_hi[0:Q, :], by_tile(drow), AX, ALU.max).then_inc(s_tiles, 1)
            dve.wait_ge(s_tiles, 2)
            own(v.tensor_reduce(base_f[0:Q, :], tile_lo[0:Q, :].rearrange("q (s t) -> q s t", t=T), AX, ALU.min))
            dve.wait_ge(s_src, 16)
            own(ts(raw.bitcast(I32), rawf.bitcast(I32), 2, None, ALU.logical_shift_right))
            own(v.tensor_copy(prow, raw.bitcast(I32)))
            own(ts(raw.bitcast(I32), rawf.bitcast(I32), J - 1, None, ALU.bitwise_and))
            own(v.tensor_copy(arow, raw.bitcast(I32)))
            own(v.tensor_copy(rel_row, rawf.bitcast(I32)))
            own(v.tensor_copy(rawf, rel_row))
            own(ts(raw, prow, 1.0 / CP, 0.5 / CP - 0.5, ALU.mult, ALU.add))
            own(ts(raw, raw, ROUND, None, ALU.add))
            own(ts(raw, raw, ROUND, None, ALU.subtract))
            own(v.scalar_tensor_tensor(out=arow, in0=raw, scalar=float(J), in1=arow, op0=ALU.mult, op1=ALU.add))
            own(v.scalar_tensor_tensor(out=prow, in0=raw, scalar=-float(CP), in1=prow, op0=ALU.mult, op1=ALU.add))

            dve.wait_ge(s_tiles_ld, 32)
            rows_used = 0
            spans = row_work[:, 0:NU + G + NG + NB]
            least = row_work[:, NU + G + NG + NB:2 * (NU + G + NG + NB)]
            sets = [(r.first_tile, r.blocks * r.units, r.k, r.w) for r in regions] + [(TD, G, T, WIN), (0, NG, T, WIN)]
            starts = []
            for first, n, k, w in sets:
                view = lambda a: a[:, first:first + n * k].rearrange("o (n k) -> o n k", k=k)
                at = slice(rows_used, rows_used + n)
                own(v.tensor_reduce(least[:, at], view(lo_row), AX, ALU.min))
                own(v.tensor_reduce(spans[:, at], view(hi_row), AX, ALU.max))
                own(v.tensor_tensor(spans[:, at], spans[:, at], least[:, at], ALU.subtract))
                own(ts(spans[:, at], spans[:, at], float(w - 1), None, ALU.subtract))
                starts.append(rows_used)
                rows_used += n
            for r, at in zip(regions, starts):
                units = least[:, at:at + r.blocks * r.units].rearrange("o (b u) -> o b u", u=r.units)
                to = slice(rows_used + r.first_block, rows_used + r.first_block + r.blocks)
                own(v.tensor_reduce(least[:, to], units, AX, ALU.min))
                own(v.tensor_reduce(spans[:, to], units, AX, ALU.max))
                own(v.tensor_tensor(spans[:, to], spans[:, to], least[:, to], ALU.subtract))
                own(ts(spans[:, to], spans[:, to], float(COLS - r.w), None, ALU.subtract))
            own(v.tensor_reduce(flag_f[0:1, 0:1], spans, AX, ALU.max))
            own(ts(flag_f[0:1, 1:2], flag_f[0:1, 0:1], 0.0, None, ALU.is_le))
            own(ts(flag_f[0:1, 2:3], flag_f[0:1, 1:2], NR - 1.0, 1.0, ALU.mult, ALU.add))
            ts(flag_f[0:1, 3:4], flag_f[0:1, 1:2], -1.0, 1.0, ALU.mult, ALU.add).then_inc(s_flag_w, 1)
            own(ts(least, least, flag_f[0:1, 1:2], None, ALU.mult))
            for (first, n, k, w), at in zip(sets[:-1], starts):
                own(v.tensor_copy(hi_row[:, first:first + n * k].rearrange("o (n k) -> o n k", k=k),
                                  least[:, at:at + n].unsqueeze(2).to_broadcast([1, n, k])))
            dve.sem_inc(s_tbase, 1)
            for r, at in zip(regions, starts):
                own(v.tensor_copy(ubase[:, r.first_base:r.first_base + r.blocks * r.padded]
                                  .rearrange("o (b u) -> o b u", u=r.padded)[:, :, 0:r.units],
                                  least[:, at:at + r.blocks * r.units].rearrange("o (b u) -> o b u", u=r.units)))
            own(v.tensor_copy(gbase[:, 0:G], least[:, starts[-2]:starts[-2] + G]))
            own(v.tensor_copy(bbase, least[:, rows_used:rows_used + NB]))
            dve.sem_inc(s_bases, 1)
            dve.wait_ge(s_flag_b, 1)
            own(v.tensor_copy(flag_b[:, 0:3], ps[7][:, 0:3]))
            own(ts(base_f[0:Q, :], base_f[0:Q, :], flag_b[0:Q, 0:1], None, ALU.mult))
            v.tensor_tensor(rel_row.rearrange("q (s e) -> q s e", e=GE), drow.rearrange("q (s e) -> q s e", e=GE),
                            base_f[0:Q, :].unsqueeze(2).to_broadcast([Q, S, GE]), ALU.subtract).then_inc(s_row, 1)
            dve.wait_ge(s_tbase_ld, 16)
            own(v.tensor_tensor(by_tile(drow), by_tile(drow), tile_base[0:Q, :].unsqueeze(2).to_broadcast([Q, TR, P]), ALU.subtract))
            own(ts(arow, arow, flag_b[0:Q, 0:1], None, ALU.mult))
            v.scalar_tensor_tensor(out=arow, in0=drow, scalar=flag_b[0:Q, 1:2], in1=arow, op0=ALU.mult, op1=ALU.add).then_inc(s_row, 1)
            own(ts(prow, prow, flag_b[0:Q, 0:1], None, ALU.mult))
            own(v.scalar_tensor_tensor(out=prow, in0=rawf, scalar=flag_b[0:Q, 2:3], in1=prow, op0=ALU.mult, op1=ALU.add))
            dve.sem_inc(s_row, 3)
            dve.wait_ge(s_bases_st, 16)
            own(v.tensor_copy(base0[:, :, 0:BG], least[:, starts[-1]:starts[-1] + NG].rearrange("o (c g) -> o c g", g=BG)))
            own(v.tensor_copy(iota_run[:], iota[:]))
            dve.sem_inc(w_iota, 1)
            v.tensor_copy(flag[:], flag_f[0:1, 1:2]).then_inc(s_flag, 1)
            dve.wait_ge(s_flag, 1)
            covered = dve.value_load(flag[0:1, 0:1], min_val=0, max_val=1)

            def centre(n, rows, centred):
                own(v.tensor_reduce(stat[0:CP, 0, :], rows3(rows), AX, ALU.add))
                own(ts(stat[0:CP, 0, :], stat[0:CP, 0, :], 1.0 / D, None, ALU.mult))
                v.tensor_tensor(rows3(centred), rows3(rows), wide(stat[0:CP, 0, :]), ALU.subtract).then_inc(s_sq_in, 1)
                dve.wait_ge(s_sq, n + 1)
                v.tensor_reduce(stat[0:CP, 1, :], rows3(sq), AX, ALU.add).then_inc(s_var, 1)
                dve.wait_ge(s_root, n + 1)
                own(v.reciprocal(stat[0:CP, 2, :], stat[0:CP, 2, :]))

            def normed_relu():
                v.scalar_tensor_tensor(out=rows3(hrows), in0=rows3(hrows), scalar=0.0, in1=wide(stat[0:CP, 2, :]),
                                       op0=ALU.max, op1=ALU.mult).then_inc(s_h, 1)

            dve.wait_ge(s_x, 16)
            dve.wait_ge(s_turned, len(pieces))
            centre(0, xrows, hrows)
            normed_relu()
            own(v.memset(agg_h[0:D, :], 0.0))
            dve.wait_ge(s_resid_st, 16)
            dve.wait_ge(s_ht, NC)
            own(v.memset(deg, 0.0))
            for done in (s_add0, w_add, s_deg, w_deg, s_dadd):
                dve.sem_inc(done, 1)
            dve.sem_inc(s_add, 2)

            def one_hot(slot, values, numbers, done):
                v.tensor_tensor(onehot[:, slot, :, :], numbers[:, :].unsqueeze(1).to_broadcast([P, T, WIN]),
                                values.unsqueeze(2).to_broadcast([P, T, WIN]), ALU.is_equal).then_inc(done, 1)

            def add(at, n, bank, col, done, to=None):
                to = agg_h[0:D, :] if to is None else to
                v.tensor_tensor(to[:, bass.ds(at, n)], to[:, bass.ds(at, n)],
                                ps[bank][0:to.shape[0], col:col + n], ALU.add).then_inc(done, 1)

            def bases_of(row, first, n):
                return nc.values_load_multi_w_load_instructions(
                    row[0:1, bass.ds(first, n)], engines=[mybir.EngineType.DVE], min_val=0, max_val=N - 1,
                    skip_runtime_bounds_check_because="a base is one of dst")[1]

            def all_windows(n, table, with_deg):
                with dve.Fori(0, NG) as g:
                    dve.wait_ge(w_iota, (g + n * NG) * (NWIN + 1) + 1)
                    v.tensor_copy(iota_run[:], iota[:]).then_inc(w_iota, 1)
                    with dve.Fori(0, NWIN) as k:
                        at = (g + n * NG) * NWIN + k
                        dve.wait_ge(w_iota, (g + n * NG) * (NWIN + 1) + k + 2)
                        one_hot(0, table[:, bass.ds(g * T, T)], iota_run, w_oh)
                        dve.wait_ge(w_mm, at + 1)
                        dve.wait_ge(w_add, at + 1)
                        add(k * WIN, WIN, 0, 0, w_add)
                        if with_deg:
                            dve.wait_ge(w_deg, at + 1)
                            add(k * WIN, WIN, 0, WIN, w_deg, deg)
                        dve.wait_ge(w_oh, at + 1)
                        ts(iota_run[:], iota_run[:], float(WIN), None, ALU.add).then_inc(w_iota, 1)
                dve.wait_ge(w_add, (n + 1) * NG * NWIN + 1)
                if with_deg:
                    dve.wait_ge(w_deg, NG * NWIN + 1)

            with dve.If(covered == 1):
                with dve.Fori(0, NIT) as i:
                    for m in range(BODY + LAG):
                        if m < BODY:
                            one_hot(m % OH_SLOTS, rel0[:, bass.ds((i * BODY + m) * T, T)], iota, s_oh)
                        if m < LAG:
                            continue
                        a = m - LAG
                        if a % BG == 0:
                            base = bases_of(bases, (i * (BODY // BG) + a // BG) * 8, BG)
                        dve.wait_ge(s_mm, i * BODY + (a + 1))
                        dve.wait_ge(s_add0, i * BODY + (a + 1))
                        add(base[a % BG], WIN, a % 5, 0, s_add0)
                        dve.wait_ge(s_deg, i * BODY + (a + 1))
                        add(base[a % BG], WIN, a % 5, WIN, s_deg, deg)
                dve.wait_ge(s_add0, NG + 1)
                dve.wait_ge(s_deg, NG + 1)
            with dve.Else():
                all_windows(0, rel0, True)
            dve.sem_inc(s_pass, 1)
            dve.wait_ge(s_ub, 16 * len(regions))
            for r, ub, to in zip(regions, unit_bases, nodes):
                own(v.memset(to, -1.0))
                own(v.tensor_copy(ub, ub.bitcast(I32)))
                low = stat[0:r.blocks, 0, 0:1]
                own(v.tensor_reduce(low, ub[:, 0:r.units], AX, ALU.min))
                own(ts(ub, ub, low, None, ALU.subtract))
                own(v.tensor_tensor(to[:, 0:r.units * r.w].rearrange("b (u d) -> b u d", d=r.w),
                                    ub[:, 0:r.units].unsqueeze(2).to_broadcast([r.blocks, r.units, r.w]),
                                    iota[0:r.blocks, 0:r.w].unsqueeze(1).to_broadcast([r.blocks, r.units, r.w]), ALU.add))
            dve.sem_inc(s_nodes, 1)
            dve.wait_ge(s_deg_ld, 16)
            own(ts(degs[0:CP, :], degs[0:CP, :], 1.0, None, ALU.max))
            v.reciprocal(degs[0:CP, :], degs[0:CP, :]).then_inc(s_dinv, 1)
            dve.wait_ge(s_w, 16 * N_W)
            for k in range(NC):
                dve.wait_ge(s_m3, k + 1)
                v.tensor_tensor(yrows[:, k * J * D:(k + 1) * J * D].rearrange("p (j f) -> p j f", f=D),
                                ps[4 + k % 2][0:CP, 0:J * D].rearrange("p (j f) -> p j f", f=D),
                                brow[0:CP, 0:1, :].to_broadcast([CP, J, D]), ALU.add).then_inc(s_y, 1)
            dve.wait_ge(s_y, NC)
            centre(1, yrows, yrows)
            own(v.tensor_tensor(rows3(yrows), rows3(yrows), wide(stat[0:CP, 2, :]), ALU.mult))
            own(v.tensor_tensor(rows3(yrows), rows3(yrows), feat(1), ALU.mult))
            dve.wait_ge(s_resid_ld, 16)
            own(v.tensor_tensor(yrows, yrows, xrows, ALU.add))
            centre(2, yrows, hrows)
            normed_relu()
            own(v.memset(agg_h[0:D, :], 0.0))
            dve.wait_ge(s_hi, 1)
            v.tensor_tensor(rows3(xrows), rows3(hrows), parts[:, :, 0, :], ALU.subtract).then_inc(s_t, 1)
            dve.wait_ge(s_mid, 1)
            v.tensor_tensor(parts[:, :, 2, :], rows3(xrows), parts[:, :, 1, :], ALU.subtract).then_inc(s_parts, 1)
            dve.wait_ge(s_parts, 1)
            dve.wait_ge(s_tab, 16)
            dve.wait_ge(s_ht, 2 * NC)
            for c in range(2):
                own(v.memset(counts[c][:, min(r.units * r.w for r in regions):COLS, :], 0.0))
            dve.sem_inc(s_zero, 1)
            dve.wait_ge(s_bases_ld, 16)
            dve.wait_ge(s_node_at, 1)

            def output_rows(k):
                n = 2 * NC + k
                dve.wait_ge(s_conv, n + 1)
                dve.wait_ge(s_res[k % 2], 16 * (k // 2 + 1))
                stored(dve, n)
                v.tensor_tensor(stage[0:CP, n % 2, :], ps[k % 2][0:CP, 0:J * D], resid[0:CP, k % 2, :], ALU.add).then_inc(s_o, 1)

            for layer in range(3):
                def group_one_hot(g, s):
                    one_hot(s, key[:, bass.ds(g * T + TD, T)], iota, s_goh)

                def group_add(g, s, base, blocks):
                    dve.wait_ge(s_win, g + (layer * G + 1 + GSLOT))
                    dve.wait_ge(s_add, g + (layer * G + 2))
                    dve.wait_ge(s_dadd, blocks + (layer * NB + 1))
                    add(base, WIN, WBANK + s % 2, 0, s_add)

                def unit_one_hots(r, b, u, c):
                    nq = len(r.quanta)
                    dve.wait_ge(s_built, b * (r.units * nq) + (r.first_quantum + u * nq + 1))
                    oh = unit_oh[(u + c * r.units) % 2]
                    for t in range(r.k):
                        tile = b * (r.units * r.k) + (r.first_tile + u * r.k + t)
                        ts(oh[:, KW * NR + t * P:KW * NR + t * P + CP], iota16[:, 0:CP], who[:, bass.ds(tile, 1)], None, ALU.is_equal)
                        ins = ts(oh[:, t * r.w * NR:(t + 1) * r.w * NR], iota16[:, 0:r.w * NR], key[:, bass.ds(tile, 1)],
                                 None, ALU.is_equal)
                    ins.then_inc(s_unit, 1)

                def block_add(r, b, groups):
                    dve.wait_ge(s_tr, b + (layer * NB + r.first_block + 2))
                    dve.wait_ge(s_add, groups + (layer * G + 2))
                    dve.wait_ge(s_dadd, b + (layer * NB + r.first_block + 1))
                    base = bases_of(bases, b + (BBASE + r.first_block), 1)[0]
                    add(base, COLS, TURN, 0, s_dadd)

                def selection(r, b):
                    ts(sel[:], iota16[:, 0:COLS], node_at[:, bass.ds(b + r.first_block, 1)], None, ALU.is_equal).then_inc(s_sel, 1)

                def step(r, built, multiplied, c):
                    if multiplied is not None:
                        selection(r, multiplied)
                    if built is not None:
                        g = (built + r.first_block) * 2
                        s = 2 * c
                        blocks = r.first_block if multiplied is None else multiplied + r.first_block
                        for ahead in range(2, 4):
                            group_one_hot(g + ahead, (s + ahead) % GSLOT)
                        if layer == 0:
                            for u in range(r.units // 2 + 1):
                                unit_one_hots(r, built, u, c)
                        base = bases_of(bases, g + NBASE, 2)
                        group_add(g, s, base[0], blocks)
                        if layer == 0:
                            for u in range(r.units // 2 + 1, r.units):
                                unit_one_hots(r, built, u, c)
                        group_add(g + 1, s + 1, base[1], blocks)
                        groups = g + 2
                    else:
                        groups = 2 * (r.first_block + r.blocks)
                    if multiplied is not None:
                        block_add(r, multiplied, groups)

                def group(g, s):
                    if not isinstance(g, int) or g + 2 < G:
                        group_one_hot(g + 2, (s + 2) % GSLOT)
                    group_add(g, s, bases_of(bases, g + NBASE, 1)[0], NB)

                with dve.If(covered == 1):
                    for g in range(2):
                        group_one_hot(g, g)
                    walk(dve, layer, step, group)
                    dve.wait_ge(s_add, (layer + 1) * G + 2)
                    dve.wait_ge(s_dadd, (layer + 1) * NB + 1)
                with dve.Else():
                    all_windows(layer + 1, key, False)
                for k in range(NC):
                    n = layer * NC + k
                    dve.wait_ge(s_dchunk[n % 2], 16 * (n // 2 + 1))
                    v.tensor_tensor(agg_h[0:D, cidx(k)], agg_h[0:D, cidx(k)], dinv[:, n % 2, :], ALU.mult).then_inc(s_scaled, 1)
                    if k >= 1:
                        after_conv(dve, layer, k - 1, output_rows, own)
                after_conv(dve, layer, NC - 1, output_rows, own)


_INS = ['x', 'src', 'dst', 'edge_attr_64', 'L0_gnn_W0', 'L0_gnn_b0', 'L0_gnn_W1', 'L0_gnn_b1', 'L0_gnn_W2', 'L0_gnn_b2',
        'L0_gnn_ln_g', 'L0_gnn_ln_b', 'L1_gnn_W1l', 'L1_gnn_b1', 'L1_gnn_W1r', 'L1_gnn_W2l', 'L1_gnn_b2', 'L1_gnn_W2r',
        'L1_gnn_W3l', 'L1_gnn_b3', 'L1_gnn_W3r']


def kernel(**inputs):
    import concourse.bacc as bacc
    from concourse.bass_utils import run_bass_kernel_spmd

    nc = bacc.Bacc("TRN2", target_bir_lowering=False, num_devices=1)
    arrays, args = {}, []
    for name in _INS:
        a = np.ascontiguousarray(inputs[name])
        arrays[f"in_{name}"] = a
        args.append(nc.dram_tensor(f"in_{name}", a.shape, mybir.dt.from_np(a.dtype), kind="ExternalInput").ap())
    args.append(nc.dram_tensor("out_x", inputs['x'].shape, F32, kind="ExternalOutput").ap())
    gnn_kernel(nc, *args)
    r = run_bass_kernel_spmd(nc, [arrays], core_ids=[0])
    return r.results[0]["out_x"]
```

```python
from contextlib import ExitStack
from math import ceil, sqrt

import numpy as np

import concourse.bass as bass
from concourse import mybir

F32 = mybir.dt.float32
BF16 = mybir.dt.bfloat16
F16 = mybir.dt.float16
I32 = mybir.dt.int32
U8 = mybir.dt.uint8
ALU = mybir.AluOpType
ACT = mybir.ActivationFunctionType
AX = mybir.AxisListType.X

P = 128
D = 64
HID = 128
EPS = 1e-5
T = 5
GE = T * P
BG = 5
RING = 5
BODY = 25
WIN = 64
OH_SLOTS = 5
LAG = 2
CP, J = 125, 4
CH = CP * J
COLS = 128
GSLOT = 4
STAGES = 4
ROUND = 12582912.0


class Region:

    def __init__(self, k, w, units, first_tile, first_block, first_unit, first_quantum, first_base):
        self.k, self.w, self.units, self.pairs = k, w, units, 0
        self.first_tile, self.first_block, self.first_unit = first_tile, first_block, first_unit
        self.first_quantum, self.first_base = first_quantum, first_base
        self.padded = 4 * ceil(units / 4)
        half = ceil(w / 2)
        self.quanta = [half] if half <= 5 else [ceil(half / 2), half - ceil(half / 2)]
        assert w % 2 == 0 and half <= 10

    tiles = property(lambda self: 2 * self.pairs * self.units * self.k)
    blocks = property(lambda self: 2 * self.pairs)


def plan(n_nodes, n_edges):
    n_tiles = n_edges // P
    regions, t, b, u, q, s = [], 0, 0, 0, 0, 0
    while True:
        k = 2
        w, end = 2, t
        while True:
            w += 2
            units = COLS // w
            end = t + 2 * units * k
            pos = end / n_tiles
            per_tile = 2 * P * n_nodes * pos / n_edges
            if 1 + per_tile * k + 5 * sqrt(per_tile * k * n_nodes * 2 * pos / n_edges) <= w:
                break
        if (n_tiles - end) / T < 2 * (b + 2) + 6:
            units = max(x for x in range(units) if (n_tiles - t - 2 * x * k) % T == 0
                        and (n_tiles - t - 2 * x * k) / T >= (2 * (b + 2) + 3 if x else 2 * b + 3))
            if units:
                regions.append(Region(k, w, units, t, b, u, q, s))
                regions[-1].pairs = 1
            return regions
        if not regions or (regions[-1].k, regions[-1].w) != (k, w):
            regions.append(Region(k, w, units, t, b, u, q, s))
        r = regions[-1]
        r.pairs += 1
        t, b, u = end, b + 2, u + 2 * units
        q += 2 * units * len(r.quanta)
        s += 2 * r.padded


def gnn_kernel(nc, x, src, dst, edge_attr, W0, b0, W1, b1, W2, b2, ln_g, ln_b,
               W1l, c1, W1r, W2l, c2, W2r, W3l, c3, W3r, out):
    N = x.shape[0]
    E = src.shape[0]
    NT = E // P
    NG = E // GE
    Q = max(q for q in range(1, P + 1) if NG % q == 0)
    S = NG // Q
    TR = S * T
    NC = N // CH
    NR = NC * J
    NIT = NG // BODY
    NWIN = -(-N // WIN)
    WIDE = (NWIN + COLS // WIN) * WIN
    RE = TR * P

    regions = plan(N, E)
    last = regions[-1]
    TD = last.first_tile + last.tiles
    NB = last.first_block + last.blocks
    NU = last.first_unit + last.blocks * last.units
    NQ = last.first_quantum + last.blocks * last.units * len(last.quanta)
    NBASE = last.first_base + last.blocks * last.padded
    G = (NT - TD) // T
    BBASE = NBASE + 4 * ceil(G / 4)
    ALL_BASES = BBASE + NB
    PAIRED = 2 * NB
    REST4 = (G - PAIRED - 3) // 4
    REST = PAIRED + 4 * REST4
    WMAX = max(r.w for r in regions)
    KW = max(r.k * r.w for r in regions)
    KMAX = max(r.k for r in regions)
    assert N % CH == 0 and E % GE == 0 and NG % BODY == 0 and (NT - TD) % T == 0 and G >= PAIRED + 3
    assert WMAX * NR <= 2048 and KMAX * P <= 256 and 2 * (NU + G + NG + NB) <= NR * D
    OHB = KW * NR + KMAX * P
    slot_uses = [len(range(s, G, GSLOT)) for s in range(GSLOT)]

    with ExitStack() as ctx:
        def sb(name, shape, dt=F32):
            return ctx.enter_context(nc.sbuf_tensor(name, shape, dt))

        def sem(name):
            return ctx.enter_context(nc.semaphore(name))

        agg_h = sb("agg_h", [P, max(WIDE, 3 * RE, NR * D)])
        NRD = NR * D
        CB = COLS * NR // 2
        big = sb("big", [P, max(2 * CB + 3 * NRD // 2, 3 * NRD + 4 * CH, max(WIDE, 2 * NRD) + RING * T * D, 2 * NRD + 3 * RE,
                                2 * NRD + RING * T * D)])
        hrows = big[0:CP, 0:NRD]
        xrows = big[0:CP, NRD:2 * NRD]
        yrows = big[0:CP, 2 * NRD:3 * NRD]
        hid_v = big[:, 3 * NRD:3 * NRD + 4 * CH].rearrange("p (l s c) -> p l s c", l=2, s=2)
        deg = big[0:1, 0:WIDE]
        rat = max(WIDE, 2 * NRD)
        ring = big[:, rat:rat + RING * T * D].rearrange("p (s r) -> p s r", s=RING)
        counts = [big[0:CP, i * CB:(i + 1) * CB].bitcast(BF16).rearrange("p (d a) -> p d a", a=NR) for i in range(2)]
        parts = big[0:CP, 2 * CB:2 * CB + 3 * NRD // 2].bitcast(BF16).rearrange("p (a s f) -> p a s f", s=3, f=D)
        key = sb("key", [P, NT])
        who = sb("who", [P, NT])
        scratch = sb("scratch", [P, max(NT, OHB, 10 * J * D)])
        rel0 = scratch[:, 0:NT]
        unit_oh = [scratch[:, i * OHB // 2:(i + 1) * OHB // 2].bitcast(BF16) for i in range(2)]
        chunk_rows = scratch[:, 0:10 * J * D].rearrange("p (i r) -> p i r", i=10)
        stage, resid, left = chunk_rows[:, 0:STAGES, :], chunk_rows[:, 4:6, :], chunk_rows[:, 6:6 + STAGES, :]
        gring = sb("gring", [P, GSLOT, T, D])
        idx = sb("idx", [P, GSLOT, T], I32)
        onehot = sb("onehot", [P, OH_SLOTS, T, WIN])
        iota = sb("iota", [P, WIN])
        iota_run = sb("iota_run", [P, WIN])
        iota16 = sb("iota16", [P, max(P, WMAX * NR)], F16)
        ident = sb("ident", [P, P])
        ones = sb("ones", [P, P])
        ones16 = sb("ones16", [P, 1], BF16)
        bases = sb("bases", [1, max((NG // BG) * 8, ALL_BASES)], I32)
        base0 = bases[:, 0:(NG // BG) * 8].rearrange("o (c g) -> o c g", g=8)
        ubase = bases[:, 0:NBASE]
        gbase = bases[:, NBASE:NBASE + 4 * ceil(G / 4)]
        bbase = bases[:, BBASE:ALL_BASES]
        node_at = sb("node_at", [P, NB])
        sel = sb("sel", [P, COLS])
        spare = gring[:].rearrange("p s t f -> p (s t f)")
        assert len(regions) * (COLS + 32) <= GSLOT * T * D
        unit_bases = [spare[0:r.blocks, len(regions) * COLS + i * 32:len(regions) * COLS + i * 32 + r.padded] for i, r in enumerate(regions)]
        nodes = [spare[0:r.blocks, i * COLS:(i + 1) * COLS] for i, r in enumerate(regions)]
        base_f = sb("base_f", [P, S])
        tile_lo = sb("tile_lo", [P, TR])
        tile_hi = sb("tile_hi", [P, TR])
        tile_base = sb("tile_base", [P, TR])
        src_lo = sb("src_lo", [P, TR])
        flag_f = sb("flag_f", [1, 4])
        flag_b = sb("flag_b", [P, 4])
        flag = sb("flag", [1, 1], I32)
        w0 = sb("w0", [P, HID])
        w1 = sb("w1", [HID, HID])
        w2 = sb("w2", [HID, D])
        wc = sb("wc", [P, 3, D])
        bias = sb("bias", [HID, 4])
        brow = sb("brow", [P, 4, D])
        eps = sb("eps", [P, 1])
        stat = sb("stat", [P, 3, NR])
        degs = sb("degs", [P, NR])
        dinv = sb("dinv", [D, 2, CH])
        QUARTER = COLS // 4
        QB = QUARTER * NR // 4
        assert 2 * QB <= TD
        quarter = [(key, who)[q // 2][0:CP, (q % 2) * QB:(q % 2 + 1) * QB].bitcast(U8) for q in range(4)]
        prod = sb("prod", [P, 3 * D])
        psum = ctx.enter_context(nc.psum_tensor("psum", [P, 8, 512], F32))
        ps = [psum[:, i, :] for i in range(8)]
        PROD, TURN, WBANK = 4, 5, 6

        tile_dram = nc.dram_tensor("tile_dram", [3, NT], F32).ap()
        base_dram = nc.dram_tensor("base_dram", [ALL_BASES], I32).ap()
        deg_dram = nc.dram_tensor("deg_dram", [N], F32).ap()
        dinv_dram = nc.dram_tensor("dinv_dram", [N], F32).ap()
        resid_dram = nc.dram_tensor("resid_dram", [CP, NRD], F32).ap()
        tables = [nc.dram_tensor(f"h_table{i}", [N, D], F32).ap() for i in range(3)]
        x1_dram = nc.dram_tensor("x1_dram", [N, D], F32).ap()
        count_dram = nc.dram_tensor("count_dram", [NB, CP, COLS * NR], U8).ap()

        s_go = sem("s_go")
        s_go_sp = sem("s_go_sp")
        s_w = sem("s_w")
        s_x = sem("s_x")
        s_dst = sem("s_dst")
        s_src = sem("s_src")
        s_const = sem("s_const")
        s_tiles = sem("s_tiles")
        s_tiles_st = sem("s_tiles_st")
        s_tiles_ld = sem("s_tiles_ld")
        s_tbase = sem("s_tbase")
        s_tbase_st = sem("s_tbase_st")
        s_tbase_ld = sem("s_tbase_ld")
        s_bases = sem("s_bases")
        s_bases_st = sem("s_bases_st")
        s_bases_ld = sem("s_bases_ld")
        s_ub = sem("s_ub")
        s_nodes = sem("s_nodes")
        s_nodes_t = sem("s_nodes_t")
        s_node_at = sem("s_node_at")
        s_sel = sem("s_sel")
        s_flag_w = sem("s_flag_w")
        s_flag_b = sem("s_flag_b")
        s_flag = sem("s_flag")
        s_row = sem("s_row")
        s_turn = sem("s_turn")
        s_turned = sem("s_turned")
        s_dv = sem("s_dv")
        s_sq_in = sem("s_sq_in")
        s_sq = sem("s_sq")
        s_var = sem("s_var")
        s_root = sem("s_root")
        s_h = sem("s_h")
        s_ht = sem("s_ht")
        s_hc = sem("s_hc")
        s_resid = sem("s_resid")
        s_resid_st = sem("s_resid_st")
        s_resid_ld = sem("s_resid_ld")
        s_attr = [sem(f"s_attr{i}") for i in range(RING)]
        s_oh = sem("s_oh")
        s_mm = sem("s_mm")
        s_add0 = sem("s_add0")
        s_deg = sem("s_deg")
        s_deg_all = sem("s_deg_all")
        s_deg_st = sem("s_deg_st")
        s_deg_ld = sem("s_deg_ld")
        s_dinv = sem("s_dinv")
        s_dinv_st = sem("s_dinv_st")
        s_pass = sem("s_pass")
        s_m1 = sem("s_m1")
        s_a1 = sem("s_a1")
        s_m2 = sem("s_m2")
        s_a2 = sem("s_a2")
        s_m3 = sem("s_m3")
        s_y = sem("s_y")
        s_x1 = sem("s_x1")
        s_x1_st = sem("s_x1_st")
        s_tab = sem("s_tab")
        s_hi = sem("s_hi")
        s_t = sem("s_t")
        s_mid = sem("s_mid")
        s_parts = sem("s_parts")
        s_zero = sem("s_zero")
        s_idx = sem("s_idx")
        s_rows = [sem(f"s_rows{i}") for i in range(GSLOT)]
        s_goh = sem("s_goh")
        s_win = sem("s_win")
        s_add = sem("s_add")
        s_unit = sem("s_unit")
        s_built = sem("s_built")
        s_banks = sem("s_banks")
        s_stored = sem("s_stored")
        s_count_st = sem("s_count_st")
        s_quarter = [sem(f"s_quarter{q}") for q in range(4)]
        s_cvd = sem("s_cvd")
        s_cva = sem("s_cva")
        s_mul = sem("s_mul")
        s_prod = sem("s_prod")
        s_tr = sem("s_tr")
        s_dadd = sem("s_dadd")
        s_scaled = sem("s_scaled")
        s_dchunk = [sem("s_dchunk0"), sem("s_dchunk1")]
        s_conv = sem("s_conv")
        s_clear = sem("s_clear")
        s_act = sem("s_act")
        s_tp = sem("s_tp")
        s_stage = sem("s_stage")
        s_store = [sem(f"s_store{i}") for i in range(STAGES)]
        s_res = [sem("s_res0"), sem("s_res1")]
        s_o = sem("s_o")
        w_row = sem("w_row")
        w_rows = sem("w_rows")
        w_idx = sem("w_idx")
        w_oh = sem("w_oh")
        w_mm = sem("w_mm")
        w_add = sem("w_add")
        w_iota = sem("w_iota")
        w_deg = sem("w_deg")

        cidx = lambda k: slice(k * CH, (k + 1) * CH)
        N_W = 18

        def column(rows, k, j):
            return agg_h[rows, k * CH + j:(k + 1) * CH:J]

        def table_chunk(t, k):
            return t[k * CH:(k + 1) * CH, :].rearrange("(p j) f -> p (j f)", j=J)

        attr_v = edge_attr.rearrange("(g p t) f -> g p (t f)", p=P, t=T)
        tile_of = ring.rearrange("p s (t f) -> p s t f", f=D)
        drow, arow, prow = (agg_h[0:Q, i * RE:(i + 1) * RE] for i in range(3))
        raw, rawf, rel_row = (big[0:Q, 2 * NRD + i * RE:2 * NRD + (i + 1) * RE] for i in range(3))
        by_tile = lambda a: a.rearrange("q (c e) -> q c e", e=P)
        lo_row, hi_row = key[0:1, :], who[0:1, :]
        row_work = big[0:1, 0:2 * (NU + G + NG + NB)]
        sq = agg_h[0:CP, 0:NRD]
        rows3 = lambda a: a.rearrange("p (r f) -> p r f", f=D)
        wide = lambda a: a.unsqueeze(2).to_broadcast([CP, NR, D])
        feat = lambda i: brow[0:CP, i:i + 1, :].to_broadcast([CP, NR, D])
        table_v = lambda c: c.rearrange("p (q c) -> p q c", c=TR)
        turns = [(rel_row, "strided", table_v(rel0)),
                 (arow, "dense", table_v(key[:])), (drow, "gathered", table_v(key[:])),
                 (prow, "dense", table_v(who[:])), (rawf, "gathered", table_v(who[:]))]

        def rows_of(kind, c):
            edge = min(Q, max(0, ceil((TD - c) / TR)))
            return {"strided": (0, Q), "dense": (0, edge), "gathered": (edge, Q)}[kind]

        pieces = [(n, c) for n, (_, kind, _) in enumerate(turns) for c in range(TR)
                  if rows_of(kind, c)[0] < rows_of(kind, c)[1]]

        def stored(eng, n):
            if n >= STAGES:
                eng.wait_ge(s_store[n % STAGES], 16 * (n // STAGES))

        def load_attr(sp, s, group, landed):
            sp.dma_start(ring[:, s, :], attr_v[bass.ds(group, 1)].rearrange("o p r -> (o p) r")).then_inc(landed, 16)

        def store_out(sp, k):
            n = 2 * NC + k
            sp.wait_ge(s_o, k + 1)
            sp.dma_start(table_chunk(out, k), stage[0:CP, n % STAGES, :]).then_inc(s_store[n % STAGES], 16)

        def load_dinv(sp, n):
            if n >= 2:
                sp.wait_ge(s_scaled, n - 1)
            k = n % NC
            sp.dma_start(dinv[:, n % 2, :], dinv_dram[cidx(k)].rearrange("(o c) -> o c", o=1).to_broadcast([D, CH])
                         ).then_inc(s_dchunk[n % 2], 16)

        def to_bf16(eng, layer, b, c, q):
            eng.wait_ge(s_quarter[q], b * 16 + ((layer - 1) * NB + 1) * 16)
            eng.wait_ge(s_mul, b + (layer * NB + 1))
            copy, done = (nc.scalar.copy, s_cva) if q == 3 else (nc.vector.tensor_copy, s_cvd)
            copy(counts[c][:, q * QUARTER:(q + 1) * QUARTER, :], quarter[q].rearrange("p (d a) -> p d a", a=NR)).then_inc(done, 1)

        def next_block(r, b):
            n = b + (r.first_block + 1)
            return None if isinstance(n, int) and n == NB else n

        def copy_h(eng, copy, n, chunks):
            for k in chunks:
                eng.wait_ge(s_ht, n * NC + k + 1)
                if k >= 1:
                    eng.wait_ge(s_hc, n * NC + k)
                copy(agg_h[D:2 * D, cidx(k)].rearrange("f (p j) -> f j p", j=J),
                               ps[4 + k % 2][0:D, 0:CH].rearrange("f (j p) -> f j p", j=J)).then_inc(s_hc, 1)

        def transpose_h(pe, n):
            pe.wait_ge(s_h, n + 1)
            for k in range(NC):
                if k >= 2:
                    pe.wait_ge(s_hc, n * NC + k - 1)
                for j in range(J):
                    r = k * J + j
                    mm = nc.tensor.transpose(ps[4 + k % 2][0:D, j * CP:(j + 1) * CP], hrows[:, r * D:(r + 1) * D],
                                             ident[0:CP, 0:CP])
                mm.then_inc(s_ht, 1)

        def walk(eng, layer, step, group):
            for r in regions:
                if layer == 0:
                    step(r, 0, None, 0)
                    if r.pairs > 1:
                        with eng.Fori(0, r.pairs - 1) as i:
                            step(r, 2 * i + 1, 2 * i, 1)
                            step(r, 2 * i + 2, 2 * i + 1, 0)
                    step(r, r.blocks - 1, r.blocks - 2, 1)
                    step(r, None, r.blocks - 1, 0)
                else:
                    loop = r.pairs - (r is last)
                    if loop:
                        with eng.Fori(0, loop) as i:
                            step(r, 2 * i, 2 * i, 0)
                            step(r, 2 * i + 1, 2 * i + 1, 1)
                    if r is last:
                        step(r, 2 * loop, 2 * loop, 0)
                        step(r, 2 * loop + 1, 2 * loop + 1, 1)
            if REST4:
                with eng.Fori(0, REST4) as i:
                    for s in range(4):
                        group(PAIRED + s + 4 * i, s)
            for g in range(REST, G):
                group(g, g % GSLOT)

        block = ctx.enter_context(nc.Block())

        @block.sync
        def _(sp):
            sp.dma_start(raw.bitcast(I32), dst.rearrange("(q n) -> q n", q=Q)).then_inc(s_dst, 16)
            sp.dma_start(rawf.bitcast(I32), src.rearrange("(q n) -> q n", q=Q)).then_inc(s_src, 16)
            sp.dma_start(xrows.rearrange("p (k r) -> p k r", k=NC),
                         x.rearrange("(k p j) f -> p k (j f)", p=CP, j=J)).then_inc(s_x, 16)
            sp.dma_start(w0[0:D, :], W0[D:2 * D, :]).then_inc(s_w, 16)
            sp.dma_start(w0[D:2 * D, :], W0[0:D, :]).then_inc(s_w, 16)
            sp.dma_start(w1[:], W1).then_inc(s_w, 16)
            sp.dma_start(w2[:], W2).then_inc(s_w, 16)
            for i, (wl, wr) in enumerate(((W1l, W1r), (W2l, W2r), (W3l, W3r))):
                sp.dma_start(wc[0:D, i, :], wl).then_inc(s_w, 16)
                sp.dma_start(wc[D:2 * D, i, :], wr).then_inc(s_w, 16)
            for i, b in enumerate((b0, b1, c1, c2)):
                sp.dma_start(bias[0:b.shape[0], i:i + 1], b.rearrange("(p o) -> p o", o=1)).then_inc(s_w, 16)
            for i, b in enumerate((b2, ln_g, ln_b, c3)):
                sp.dma_start(brow[:, i, :], b.rearrange("(o f) -> o f", o=1).to_broadcast([P, D])).then_inc(s_w, 16)
            sp.wait_ge(s_tiles, 1)
            for i, a in enumerate((tile_lo, tile_hi)):
                sp.dma_start(tile_dram[i].rearrange("(q c) -> q c", q=Q), a[0:Q, :]).then_inc(s_tiles_st, 16)
            sp.wait_ge(s_tiles_st, 32)
            for i, a in enumerate((lo_row, hi_row)):
                sp.dma_start(a, tile_dram[i:i + 1, :]).then_inc(s_tiles_ld, 16)
            sp.wait_ge(s_tbase, 1)
            sp.dma_start(tile_dram[2:3, :], hi_row).then_inc(s_tbase_st, 16)
            sp.wait_ge(s_tbase_st, 16)
            sp.dma_start(tile_base[0:Q, :], tile_dram[2].rearrange("(q c) -> q c", q=Q)).then_inc(s_tbase_ld, 16)
            sp.wait_ge(s_bases, 1)
            sp.dma_start(base_dram.rearrange("(o n) -> o n", o=1), bases[:, 0:ALL_BASES]).then_inc(s_bases_st, 16)
            sp.wait_ge(s_bases_st, 16)
            for r, to in zip(regions, unit_bases):
                sp.dma_start(to.bitcast(I32), base_dram[r.first_base:r.first_base + r.blocks * r.padded]
                             .rearrange("(b u) -> b u", u=r.padded)).then_inc(s_ub, 16)
            sp.wait_ge(s_resid, 1)
            sp.dma_start(resid_dram, xrows).then_inc(s_resid_st, 16)

            sp.wait_ge(s_turned, len(pieces))
            sp.wait_ge(s_flag, 1)
            covered = sp.value_load(flag[0:1, 0:1], min_val=0, max_val=1)
            with sp.If(covered == 1):
                for s in range(RING):
                    load_attr(sp, s, s, s_attr[s])
                with sp.Fori(0, NIT - 1) as i:
                    for m in range(BODY):
                        sp.wait_ge(s_mm, i * BODY + (m + 1))
                        load_attr(sp, m % RING, i * BODY + (m + RING), s_attr[m % RING])
                for m in range(NG - BODY, NG - RING):
                    sp.wait_ge(s_mm, m + 1)
                    load_attr(sp, m % RING, m + RING, s_attr[m % RING])
            with sp.Else():
                with sp.Fori(0, NG) as g:
                    sp.wait_ge(w_add, g * NWIN + 1)
                    load_attr(sp, 0, g, w_row)

            sp.wait_ge(s_pass, 1)
            sp.dma_start(deg_dram.rearrange("(o n) -> o n", o=1), deg[:, 0:N]).then_inc(s_deg_st, 16)
            sp.wait_ge(s_bases_st, 16)
            sp.dma_start(bases[:, 0:ALL_BASES], base_dram.rearrange("(o n) -> o n", o=1)).then_inc(s_bases_ld, 16)
            sp.wait_ge(s_deg_st, 16)
            sp.dma_start(degs[0:CP, :], deg_dram.rearrange("(p c) -> p c", p=CP)).then_inc(s_deg_ld, 16)
            sp.wait_ge(s_resid_st, 16)
            sp.dma_start(xrows, resid_dram).then_inc(s_resid_ld, 16)
            sp.wait_ge(s_dinv, 1)
            sp.dma_start(dinv_dram.rearrange("(p c) -> p c", p=CP), degs[0:CP, :]).then_inc(s_dinv_st, 16)

            sp.wait_ge(s_x1, 1)
            sp.dma_start(x1_dram.rearrange("(k p j) f -> p k (j f)", p=CP, j=J),
                         yrows.rearrange("p (k r) -> p k r", k=NC)).then_inc(s_x1_st, 16)
            sp.wait_ge(s_h, 2)
            sp.dma_start(tables[0].rearrange("(k p j) f -> p k (j f)", p=CP, j=J),
                         hrows.rearrange("p (k r) -> p k r", k=NC)).then_inc(s_tab, 16)
            sp.wait_ge(s_dinv_st, 16)
            for layer in range(3):
                def load_block(b):
                    for q in range(4):
                        if q < 3:
                            sp.wait_ge(s_cvd, b * 3 + ((layer - 1) * NB * 3 + q + 1))
                        else:
                            sp.wait_ge(s_cva, b + ((layer - 1) * NB + 1))
                        sp.sem_inc(s_go_sp, 1)
                        sp.dma_start(quarter[q], count_dram[bass.ds(b, 1), :, q * QUARTER * NR:(q + 1) * QUARTER * NR]
                                     .rearrange("o p n -> (o p) n")).then_inc(s_quarter[q], 16)

                def count_step(r, built, multiplied, c):
                    b = next_block(r, multiplied)
                    if b is not None:
                        load_block(b)

                with sp.If(covered == 1):
                    if layer == 1:
                        sp.wait_ge(s_count_st, 16 * NB)
                    if layer > 0:
                        load_block(0)
                        walk(sp, layer, count_step, lambda g, s: None)
                    else:
                        sp.sem_inc(s_go_sp, 1)
                with sp.Else():
                    sp.sem_inc(s_go, 1)
                for n in range(2):
                    load_dinv(sp, layer * NC + n)
                if layer == 2:
                    break
                for k in range(NC):
                    n = layer * NC + k
                    if k + 2 < NC:
                        load_dinv(sp, n + 2)
                    sp.wait_ge(s_stage, n + 1)
                    sp.dma_start(table_chunk(tables[layer + 1], k), stage[0:CP, n % STAGES, :]).then_inc(s_store[n % STAGES], 16)
            sp.wait_ge(s_x1_st, 16)
            for k in range(NC):
                if k >= 2:
                    sp.wait_ge(s_o, k - 1)
                sp.dma_start(resid[0:CP, k % 2, :], table_chunk(x1_dram, k)).then_inc(s_res[k % 2], 16)
                if k >= 1:
                    store_out(sp, k - 1)
                if k + 2 < NC:
                    load_dinv(sp, 2 * NC + k + 2)
            store_out(sp, NC - 1)
            for b in range(STAGES):
                sp.wait_ge(s_store[b], 16 * len(range(b, 3 * NC, STAGES)))

        @block.gpsimd
        def _(pool):
            nc.gpsimd.memset(ident[:], 0.0).then_inc(s_const, 1)
            nc.gpsimd.iota(iota[:], pattern=[[1, WIN]], base=0, channel_multiplier=0,
                           allow_small_or_imprecise_dtypes=True).then_inc(s_const, 1)
            nc.gpsimd.iota(iota16[:], pattern=[[1, max(P, WMAX * NR)]], base=0, channel_multiplier=0,
                           allow_small_or_imprecise_dtypes=True).then_inc(s_const, 1)
            nc.gpsimd.memset(ones[:], 1.0).then_inc(s_const, 1)
            nc.gpsimd.memset(ones16[:], 1.0).then_inc(s_const, 1)
            nc.gpsimd.memset(eps[:], EPS).then_inc(s_const, 1)
            pool.wait_ge(s_const, 6)
            nc.gpsimd.affine_select(out=ident[:], in_=ident[:], compare_op=ALU.not_equal, fill=1.0, base=0,
                                    pattern=[[-1, P]], channel_multiplier=1).then_inc(s_const, 1)
            pool.wait_ge(s_var, 1)
            nc.gpsimd.memset(agg_h[0:D, :], 0.0).then_inc(s_clear, 1)
            pool.wait_ge(s_sq_in, 3)
            nc.gpsimd.tensor_tensor(rows3(yrows), rows3(yrows), feat(3), ALU.add).then_inc(s_x1, 1)
            pool.wait_ge(s_var, 3)
            nc.gpsimd.memset(agg_h[0:D, :], 0.0).then_inc(s_clear, 1)
            pool.wait_ge(s_flag, 1)
            covered = pool.value_load(flag[0:1, 0:1], min_val=0, max_val=1)
            for layer in range(3):
                if layer == 0:
                    pool.wait_ge(s_tab, 16)
                else:
                    for b in range(STAGES):
                        pool.wait_ge(s_store[b], 16 * len(range(b, layer * NC, STAGES)))
                table = tables[layer]

                def gather(slot, c, landed):
                    nc.gpsimd.indirect_dma_start(
                        out=gring[:, slot, c, :], out_offset=None, in_=table,
                        in_offset=bass.IndirectOffsetOnAxis(ap=idx[:, slot, c:c + 1], axis=0)).then_inc(landed, 16)

                def gather_group(g, s):
                    pool.wait_ge(s_idx, g + (layer * G + 1))
                    pool.wait_ge(s_win, g + (layer * G + 1))
                    pool.sem_inc(s_go, 1)
                    for c in range(T):
                        gather(s, c, s_rows[s])

                def store_step(r, built, multiplied, c):
                    if multiplied is not None:
                        b = multiplied + r.first_block
                        pool.wait_ge(s_banks, (multiplied + 1) * (r.units * len(r.quanta)) + (r.first_quantum + 2))
                        pool.sem_inc(s_go, 1)
                        nc.gpsimd.dma_start(count_dram[bass.ds(b, 1)].rearrange("o p n -> (o p) n"),
                                            counts[1 - c].rearrange("p d a -> p (d a)")).then_inc(s_count_st, 16)
                    if built is not None:
                        g = (built + r.first_block) * 2
                        for ahead in range(2, 4):
                            gather_group(g + ahead, (2 * c + ahead) % GSLOT)
                    if multiplied is not None:
                        pool.wait_ge(s_count_st, (b + 1) * 16)
                        pool.sem_inc(s_stored, 1)

                with pool.If(covered == 1):
                    if layer == 0:
                        pool.sem_inc(s_stored, 2)
                        for g in range(2):
                            gather_group(g, g)
                        walk(pool, layer, store_step, lambda g, s: gather_group(g + 2, (s + 2) % GSLOT)
                             if not isinstance(g, int) or g + 2 < G else None)
                    else:
                        with pool.Fori(0, REST // 4) as i:
                            for s in range(GSLOT):
                                gather_group(i * 4 + s, s)
                        for g in range(REST // 4 * 4, G):
                            gather_group(g, g % GSLOT)
                with pool.Else():
                    with pool.Fori(0, NG) as g:
                        pool.wait_ge(w_idx, g + (layer * NG + 1))
                        pool.wait_ge(w_add, (g + (layer + 1) * NG) * NWIN + 1)
                        pool.sem_inc(s_go, 1)
                        for c in range(T):
                            gather(0, c, w_rows)
                if layer == 2:
                    break
                for k in range(NC):
                    pool.wait_ge(s_conv, layer * NC + k + 1)
                    nc.gpsimd.memset(agg_h[0:D, cidx(k)], 0.0).then_inc(s_clear, 1)

        @block.scalar
        def _(act):
            def layernorm_roots(n):
                act.wait_ge(s_sq_in, n + 1)
                nc.scalar.activation(sq, hrows if n != 1 else yrows, ACT.Square).then_inc(s_sq, 1)
                act.wait_ge(s_var, n + 1)
                nc.scalar.activation(stat[0:CP, 2, :], stat[0:CP, 1, :], ACT.Sqrt, bias=eps[0:CP, :],
                                     scale=1.0 / D).then_inc(s_root, 1)

            act.wait_ge(s_const, 7)
            act.sem_inc(s_banks, 2)
            act.sem_inc(s_prod, 1)
            act.sem_inc(s_cva, 1)
            for m, (n, c) in enumerate(pieces):
                _, kind, to = turns[n]
                a, b = rows_of(kind, c)
                act.wait_ge(s_turn, m + 1)
                nc.scalar.copy(to[:, a:b, c], ps[m % 4][:, a:b]).then_inc(s_turned, 1)
            layernorm_roots(0)
            copy_h(act, nc.scalar.copy, 0, range(NC))
            act.wait_ge(s_flag, 1)
            covered = act.value_load(flag[0:1, 0:1], min_val=0, max_val=1)
            act.wait_ge(s_w, 16 * N_W)
            for step in range(NC + 1):
                if step < NC:
                    k = step
                    act.wait_ge(s_m1, k + 1)
                    if k >= 2:
                        act.wait_ge(s_m2, k - 1)
                    nc.scalar.activation(hid_v[:, 0, k % 2, :], ps[k % 2][:, 0:CH], ACT.Relu, bias=bias[:, 0:1]).then_inc(s_a1, 1)
                if step >= 1:
                    k = step - 1
                    act.wait_ge(s_m2, k + 1)
                    if k >= 2:
                        act.wait_ge(s_m3, k - 1)
                    nc.scalar.activation(hid_v[:, 1, k % 2, :], ps[2 + k % 2][:, 0:CH], ACT.Relu, bias=bias[:, 1:2]).then_inc(s_a2, 1)
            layernorm_roots(1)
            layernorm_roots(2)
            act.wait_ge(s_nodes_t, 1)
            nc.scalar.copy(node_at[:], ps[WBANK][:, 0:NB]).then_inc(s_node_at, 1)
            copy_h(act, nc.scalar.copy, 1, range(0, NC, 2))
            act.wait_ge(s_x1_st, 16)
            nc.scalar.copy(parts[:, :, 0, :], rows3(hrows)).then_inc(s_hi, 1)
            act.wait_ge(s_t, 1)
            nc.scalar.copy(parts[:, :, 1, :], rows3(xrows)).then_inc(s_mid, 1)
            act.wait_ge(s_zero, 1)
            for layer in range(3):
                def copy_idx(g, s):
                    act.wait_ge(s_win, g + (layer * G + 1))
                    nc.scalar.copy(idx[:, s, :], who[:, bass.ds(g * T + TD, T)]).then_inc(s_idx, 1)

                def copy_quantum(r, b, u, q, c):
                    n = r.quanta[q]
                    col = u * r.w + 2 * sum(r.quanta[:q])
                    nq = len(r.quanta)
                    at = b * (r.units * nq) + (r.first_quantum + u * nq + q)
                    pair = ((u + c * r.units) * nq + q) % 2
                    act.wait_ge(s_built, at + 3)
                    if u == 0 and q == 0:
                        act.wait_ge(s_mul, b + (r.first_block + 1))
                        act.wait_ge(s_stored, b + (r.first_block + 1))
                    nc.scalar.copy(counts[c][:, col:col + 2 * n, :].rearrange("p (h d) a -> p h (d a)", h=2),
                                   psum[0:CP, 2 * pair:2 * pair + 2, 0:n * NR]).then_inc(s_banks, 1)

                def copy_product(b):
                    act.wait_ge(s_mul, b + (layer * NB + 3))
                    act.wait_ge(s_tr, b + (layer * NB + 1))
                    nc.scalar.copy(prod[:], ps[PROD][:, 0:3 * D]).then_inc(s_prod, 1)

                def step(r, built, multiplied, c):
                    b = built if built is not None else multiplied
                    if built is not None:
                        for s in range(3, 5):
                            copy_idx((built + r.first_block) * 2 + s, (2 * c + s) % GSLOT)
                    if layer == 0:
                        for u in range(r.units if built is not None else 0):
                            for q in range(len(r.quanta)):
                                copy_quantum(r, built, u, q, c)
                            if u == r.units - 4 and multiplied is not None:
                                copy_product(multiplied + r.first_block)
                        if built is None:
                            copy_product(multiplied + r.first_block)
                    else:
                        after = next_block(r, multiplied)
                        if after is not None:
                            to_bf16(act, layer, after, 1 - c, 3)
                        copy_product(multiplied + r.first_block)

                with act.If(covered == 1):
                    for s in range(3):
                        copy_idx(s, s)
                    if layer > 0:
                        to_bf16(act, layer, 0, 0, 3)
                    walk(act, layer, step, lambda g, s: copy_idx(g + 3, (s + 3) % GSLOT) if not isinstance(g, int) or g + 3 < G else None)
                with act.Else():
                    with act.Fori(0, NG) as g:
                        act.wait_ge(w_add, (g + (layer + 1) * NG) * NWIN + 1)
                        nc.scalar.copy(idx[:, 0, :], who[:, bass.ds(g * T, T)]).then_inc(w_idx, 1)
                if layer == 2:
                    break
                for step in range(NC + 3):
                    if step < NC:
                        n = layer * NC + step
                        act.wait_ge(s_conv, n + 1)
                        nc.scalar.activation(agg_h[D:2 * D, cidx(step)], ps[step % 2][0:D, 0:CH], ACT.Relu,
                                             bias=bias[0:D, 2 + layer:3 + layer]).then_inc(s_act, 1)
                    if 1 <= step <= NC:
                        k = step - 1
                        n = layer * NC + k
                        act.wait_ge(s_tp, n + 1)
                        stored(act, n)
                        if n >= STAGES:
                            act.wait_ge(s_t, 1 + n - STAGES + 1)
                        nc.scalar.copy(stage[0:CP, n % STAGES, :], ps[2 + k % 2][0:CP, 0:J * D]).then_inc(s_stage, 1)
                        nc.scalar.copy(parts[:, k * J:(k + 1) * J, 0, :],
                                       ps[2 + k % 2][0:CP, 0:J * D].rearrange("p (j f) -> p j f", f=D)).then_inc(s_hi, 1)
                    if step >= 3:
                        k = step - 3
                        n = layer * NC + k
                        act.wait_ge(s_t, 1 + n + 1)
                        nc.scalar.copy(parts[:, k * J:(k + 1) * J, 1, :],
                                       left[0:CP, n % STAGES, :].rearrange("p (j f) -> p j f", f=D)).then_inc(s_mid, 1)

        @block.tensor
        def _(pe):
            pe.wait_ge(s_const, 7)
            pe.sem_inc(s_win, GSLOT)
            pe.sem_inc(s_built, 2)
            pe.sem_inc(s_mul, 2)
            pe.sem_inc(s_tr, 1)
            pe.wait_ge(s_flag_w, 1)
            nc.tensor.matmul(ps[7][:, 0:3], ones[0:1, :], flag_f[0:1, 1:4], start=True, stop=True).then_inc(s_flag_b, 1)
            for m, (n, c) in enumerate(pieces):
                row, kind, _ = turns[n]
                if m == 0 or pieces[m - 1][0] != n:
                    pe.wait_ge(s_row, n + 1)
                if m >= 4:
                    pe.wait_ge(s_turned, m - 3)
                cols = row[:, (c // T) * GE + c % T:(c // T + 1) * GE:T] if kind == "strided" else row[:, c * P:(c + 1) * P]
                nc.tensor.transpose(ps[m % 4][:, 0:Q], cols, ident[0:Q, 0:Q]).then_inc(s_turn, 1)
            transpose_h(pe, 0)
            pe.wait_ge(s_flag, 1)
            covered = pe.value_load(flag[0:1, 0:1], min_val=0, max_val=1)

            def window(tiles, oh, bank, done, with_deg=False):
                for t in range(T):
                    mm = nc.tensor.matmul(ps[bank][0:D, 0:WIN], tiles[:, t, :], onehot[:, oh, t, :],
                                          start=(t == 0), stop=(t == T - 1))
                if with_deg:
                    for t in range(T):
                        mm = nc.tensor.matmul(ps[bank][0:1, WIN:2 * WIN], ones16[:],
                                              onehot[:, oh, t, :].bitcast(BF16)[:, 1:2 * WIN:2],
                                              start=(t == 0), stop=(t == T - 1))
                mm.then_inc(done, 1)

            pe.wait_ge(s_turned, len(pieces))
            pe.wait_ge(s_hc, NC)
            with pe.If(covered == 1):
                with pe.Fori(0, NIT) as i:
                    for m in range(BODY):
                        pe.wait_ge(s_attr[m % RING], i * (16 * BODY // RING) + 16 * (m // RING + 1))
                        pe.wait_ge(s_oh, i * BODY + (m + 1))
                        window(tile_of[:, m % RING], m % OH_SLOTS, m % 5, s_mm, True)
            with pe.Else():
                with pe.Fori(0, NG) as g:
                    with pe.Fori(0, NWIN) as k:
                        pe.wait_ge(w_row, (g + 1) * 16)
                        pe.wait_ge(w_oh, g * NWIN + k + 1)
                        window(tile_of[:, 0], 0, 0, w_mm, True)
            pe.wait_ge(s_pass, 1)
            pe.wait_ge(s_w, 16 * N_W)
            for step in range(NC + 2):
                if step < NC:
                    k = step
                    if k >= 2:
                        pe.wait_ge(s_a1, k - 1)
                    nc.tensor.matmul(ps[k % 2][:, 0:CH], w0[:], agg_h[:, cidx(k)], start=True, stop=True).then_inc(s_m1, 1)
                if 1 <= step <= NC:
                    k = step - 1
                    pe.wait_ge(s_a1, k + 1)
                    if k >= 2:
                        pe.wait_ge(s_a2, k - 1)
                    nc.tensor.matmul(ps[2 + k % 2][:, 0:CH], w1[:], hid_v[:, 0, k % 2, :], start=True, stop=True).then_inc(s_m2, 1)
                if step >= 2:
                    k = step - 2
                    pe.wait_ge(s_a2, k + 1)
                    if k >= 2:
                        pe.wait_ge(s_y, k - 1)
                    for j in range(J):
                        mm = nc.tensor.matmul(ps[4 + k % 2][0:CP, j * D:(j + 1) * D], hid_v[:, 1, k % 2, j:CH:J], w2[:],
                                              start=True, stop=True)
                    mm.then_inc(s_m3, 1)
            pe.wait_ge(s_nodes, 1)
            for r, rows in zip(regions, nodes):
                mm = nc.tensor.transpose(ps[WBANK][:, r.first_block:r.first_block + r.blocks], rows, ident[0:r.blocks, 0:r.blocks])
            mm.then_inc(s_nodes_t, 1)
            transpose_h(pe, 1)
            pe.wait_ge(s_hc, 2 * NC)
            for layer in range(3):
                def gathered(g, s):
                    pe.wait_ge(s_rows[s], g * (4 * T) + ((1 + layer * slot_uses[s]) * 16 * T - s * 4 * T))
                    pe.wait_ge(s_goh, g + (layer * G + 1))
                    pe.wait_ge(s_add, g + (layer * G + 1))
                    window(gring[:, s], s, WBANK + s % 2, s_win)

                def build(r, b, u, c):
                    nq = len(r.quanta)
                    pe.wait_ge(s_unit, b * r.units + (r.first_unit + u + 1))
                    for q, n in enumerate(r.quanta):
                        pair = ((u + c * r.units) * nq + q) % 2
                        pe.wait_ge(s_banks, b * (r.units * nq) + (r.first_quantum + u * nq + q + 1))
                        for half in range(2):
                            col = (2 * sum(r.quanta[:q]) + half * n) * NR
                            oh = unit_oh[(u + c * r.units) % 2]
                            for t in range(r.k):
                                mm = nc.tensor.matmul(psum[0:CP, 2 * pair + half, 0:n * NR],
                                                      oh[:, KW * NR + t * P:KW * NR + t * P + CP],
                                                      oh[:, t * r.w * NR + col:t * r.w * NR + col + n * NR],
                                                      start=(t == 0), stop=(t == r.k - 1))
                        mm.then_inc(s_built, 1)

                def multiply(b, c, first, end):
                    if first == 0:
                        pe.wait_ge(s_prod, b + (layer * NB + 1))
                    for a in range(first, end):
                        mm = nc.tensor.matmul(ps[PROD][:, 0:3 * D], counts[c][:, :, a],
                                              parts[:, a, :, :].rearrange("p s f -> p (s f)"),
                                              start=(a == 0), stop=(a == NR - 1))
                    if end == NR:
                        mm.then_inc(s_mul, 1)

                def turn(r, b):
                    at = b + (layer * NB + r.first_block)
                    pe.wait_ge(s_prod, at + 2)
                    pe.wait_ge(s_dadd, b + (layer * NB + r.first_block + 1))
                    pe.wait_ge(s_sel, b + (layer * NB + r.first_block + 1))
                    for i in range(3):
                        mm = nc.tensor.matmul(ps[TURN][0:D, 0:COLS], prod[:, (2 - i) * D:(3 - i) * D], sel[:],
                                              start=(i == 0), stop=(i == 2))
                    mm.then_inc(s_tr, 1)

                def step(r, built, multiplied, c):
                    pair = None
                    if built is not None:
                        g = (built + r.first_block) * 2
                        s = 2 * c
                        gathered(g, s)
                    if layer == 0 and built is not None:
                        spread = [NR * u // (r.units - 3) for u in range(r.units - 2)]
                        for u in range(r.units):
                            build(r, built, u, c)
                            if u == 0 and multiplied is not None:
                                pe.wait_ge(s_banks, (multiplied + 1) * (r.units * len(r.quanta)) + (r.first_quantum + 2))
                            if u <= r.units - 4 and multiplied is not None:
                                multiply(multiplied + r.first_block, 1 - c, spread[u], spread[u + 1])
                            if u == r.units // 2:
                                gathered(g + 1, s + 1)
                            if u == r.units - 3 and multiplied is not None:
                                turn(r, multiplied)
                    elif layer == 0:
                        pe.wait_ge(s_banks, (multiplied + 1) * (r.units * len(r.quanta)) + (r.first_quantum + 2))
                        multiply(multiplied + r.first_block, 1 - c, 0, NR)
                        turn(r, multiplied)
                    else:
                        pe.wait_ge(s_cvd, multiplied * 3 + ((r.first_block + 2 + (layer - 1) * NB) * 3))
                        pe.wait_ge(s_cva, multiplied + (r.first_block + 2 + (layer - 1) * NB))
                        multiply(multiplied + r.first_block, c, 0, NR)
                        gathered(g + 1, s + 1)
                        turn(r, multiplied)

                if layer == 0:
                    pe.wait_ge(s_parts, 1)
                    pe.wait_ge(s_node_at, 1)
                with pe.If(covered == 1):
                    walk(pe, layer, step, gathered)
                with pe.Else():
                    with pe.Fori(0, NG) as g:
                        with pe.Fori(0, NWIN) as k:
                            pe.wait_ge(w_rows, (g + (1 + layer * NG)) * (16 * T))
                            pe.wait_ge(w_oh, (g + (layer + 1) * NG) * NWIN + k + 1)
                            window(gring[:, 0], 0, 0, w_mm)
                if layer == 2:
                    break

                def to_rows(k):
                    n = layer * NC + k
                    pe.wait_ge(s_act, n + 1)
                    if n >= 2:
                        pe.wait_ge(s_hi, 1 + n - 1)
                    for j in range(J):
                        mm = nc.tensor.transpose(ps[2 + k % 2][0:CP, j * D:(j + 1) * D], column(slice(D, 2 * D), k, j),
                                                 ident[D:2 * D, D:2 * D])
                    mm.then_inc(s_tp, 1)

                for k in range(NC):
                    n = layer * NC + k
                    pe.wait_ge(s_scaled, n + 1)
                    if n >= 2:
                        pe.wait_ge(s_act, n - 1)
                    nc.tensor.matmul(ps[k % 2][0:D, 0:CH], wc[:, layer, :], agg_h[:, cidx(k)], start=True, stop=True).then_inc(s_conv, 1)
                    if k >= 1:
                        to_rows(k - 1)
                to_rows(NC - 1)
                pe.wait_ge(s_hi, 1 + (layer + 1) * NC)
                pe.wait_ge(s_parts, 1 + (layer + 1) * NC)
            for k in range(NC):
                pe.wait_ge(s_scaled, 2 * NC + k + 1)
                if k >= 2:
                    pe.wait_ge(s_o, k - 1)
                for j in range(J):
                    mm = nc.tensor.matmul(ps[k % 2][0:CP, j * D:(j + 1) * D], column(slice(0, P), k, j), wc[:, 2, :],
                                          start=True, stop=True)
                mm.then_inc(s_conv, 1)

        @block.vector
        def _(dve):
            steps = [0]

            def own(ins):
                steps[0] += 1
                ins.then_inc(s_dv, 1)
                dve.wait_ge(s_dv, steps[0])

            v = nc.vector
            ts = v.tensor_scalar
            dve.wait_ge(s_dst, 16)
            own(v.memset(bases[:], 0))
            own(v.tensor_copy(drow, raw.bitcast(I32)))
            own(v.tensor_reduce(tile_lo[0:Q, :], by_tile(drow), AX, ALU.min))
            own(v.tensor_reduce(tile_hi[0:Q, :], by_tile(drow), AX, ALU.max))
            dve.wait_ge(s_src, 16)
            own(v.tensor_copy(rel_row, rawf.bitcast(I32)))
            own(v.tensor_reduce(tile_base[0:Q, :], by_tile(rel_row), AX, ALU.max))
            own(v.tensor_reduce(src_lo[0:Q, :], by_tile(rel_row), AX, ALU.min))
            own(v.tensor_tensor(src_lo[0:Q, :], tile_base[0:Q, :], src_lo[0:Q, :], ALU.subtract))
            own(v.tensor_tensor(src_lo[0:Q, :], src_lo[0:Q, :], tile_hi[0:Q, :], ALU.add))
            own(v.tensor_tensor(src_lo[0:Q, :], src_lo[0:Q, :], tile_lo[0:Q, :], ALU.is_equal))
            v.scalar_tensor_tensor(out=tile_hi[0:Q, :], in0=src_lo[0:Q, :], scalar=4.0 * N, in1=tile_hi[0:Q, :],
                                   op0=ALU.mult, op1=ALU.add).then_inc(s_tiles, 1)
            dve.wait_ge(s_tiles, 1)
            own(v.tensor_reduce(base_f[0:Q, :], tile_lo[0:Q, :].rearrange("q (s t) -> q s t", t=T), AX, ALU.min))
            own(ts(raw.bitcast(I32), rawf.bitcast(I32), 2, None, ALU.logical_shift_right))
            own(v.tensor_copy(prow, raw.bitcast(I32)))
            own(ts(raw.bitcast(I32), rawf.bitcast(I32), J - 1, None, ALU.bitwise_and))
            own(v.tensor_copy(arow, raw.bitcast(I32)))
            own(v.tensor_copy(rawf, rel_row))
            own(ts(raw, prow, 1.0 / CP, 0.5 / CP - 0.5, ALU.mult, ALU.add))
            own(ts(raw, raw, ROUND, None, ALU.add))
            own(ts(raw, raw, ROUND, None, ALU.subtract))
            own(v.scalar_tensor_tensor(out=arow, in0=raw, scalar=float(J), in1=arow, op0=ALU.mult, op1=ALU.add))
            own(v.scalar_tensor_tensor(out=prow, in0=raw, scalar=-float(CP), in1=prow, op0=ALU.mult, op1=ALU.add))

            dve.wait_ge(s_tiles_ld, 32)
            rows_used = 0
            spans = row_work[:, 0:NU + G + NG + NB]
            least = row_work[:, NU + G + NG + NB:2 * (NU + G + NG + NB)]
            sets = [(r.first_tile, r.blocks * r.units, r.k, r.w) for r in regions] + [(TD, G, T, WIN), (0, NG, T, WIN)]
            starts = []
            for first, n, k, w in sets:
                view = lambda a: a[:, first:first + n * k].rearrange("o (n k) -> o n k", k=k)
                at = slice(rows_used, rows_used + n)
                own(v.tensor_reduce(least[:, at], view(lo_row), AX, ALU.min))
                own(v.tensor_reduce(spans[:, at], view(hi_row), AX, ALU.max))
                own(v.tensor_tensor(spans[:, at], spans[:, at], least[:, at], ALU.subtract))
                own(ts(spans[:, at], spans[:, at], float(w - 1), None, ALU.subtract))
                starts.append(rows_used)
                rows_used += n
            for r, at in zip(regions, starts):
                units = least[:, at:at + r.blocks * r.units].rearrange("o (b u) -> o b u", u=r.units)
                to = slice(rows_used + r.first_block, rows_used + r.first_block + r.blocks)
                own(v.tensor_reduce(least[:, to], units, AX, ALU.min))
                own(v.tensor_reduce(spans[:, to], units, AX, ALU.max))
                own(v.tensor_tensor(spans[:, to], spans[:, to], least[:, to], ALU.subtract))
                own(ts(spans[:, to], spans[:, to], float(COLS - r.w), None, ALU.subtract))
            own(v.tensor_reduce(flag_f[0:1, 0:1], spans, AX, ALU.max))
            own(ts(flag_f[0:1, 1:2], flag_f[0:1, 0:1], 0.0, None, ALU.is_le))
            own(ts(flag_f[0:1, 2:3], flag_f[0:1, 1:2], NR - 1.0, 1.0, ALU.mult, ALU.add))
            ts(flag_f[0:1, 3:4], flag_f[0:1, 1:2], -1.0, 1.0, ALU.mult, ALU.add).then_inc(s_flag_w, 1)
            own(ts(least, least, flag_f[0:1, 1:2], None, ALU.mult))
            for (first, n, k, w), at in zip(sets[:-1], starts):
                own(v.tensor_copy(hi_row[:, first:first + n * k].rearrange("o (n k) -> o n k", k=k),
                                  least[:, at:at + n].unsqueeze(2).to_broadcast([1, n, k])))
            dve.sem_inc(s_tbase, 1)
            for r, at in zip(regions, starts):
                own(v.tensor_copy(ubase[:, r.first_base:r.first_base + r.blocks * r.padded]
                                  .rearrange("o (b u) -> o b u", u=r.padded)[:, :, 0:r.units],
                                  least[:, at:at + r.blocks * r.units].rearrange("o (b u) -> o b u", u=r.units)))
            own(v.tensor_copy(gbase[:, 0:G], least[:, starts[-2]:starts[-2] + G]))
            own(v.tensor_copy(bbase, least[:, rows_used:rows_used + NB]))
            dve.sem_inc(s_bases, 1)
            dve.wait_ge(s_flag_b, 1)
            own(v.tensor_copy(flag_b[:, 0:3], ps[7][:, 0:3]))
            own(ts(base_f[0:Q, :], base_f[0:Q, :], flag_b[0:Q, 0:1], None, ALU.mult))
            v.tensor_tensor(rel_row.rearrange("q (s e) -> q s e", e=GE), drow.rearrange("q (s e) -> q s e", e=GE),
                            base_f[0:Q, :].unsqueeze(2).to_broadcast([Q, S, GE]), ALU.subtract).then_inc(s_row, 1)
            dve.wait_ge(s_tbase_ld, 16)
            own(v.tensor_tensor(by_tile(drow), by_tile(drow), tile_base[0:Q, :].unsqueeze(2).to_broadcast([Q, TR, P]), ALU.subtract))
            own(ts(arow, arow, flag_b[0:Q, 0:1], None, ALU.mult))
            v.scalar_tensor_tensor(out=arow, in0=drow, scalar=flag_b[0:Q, 1:2], in1=arow, op0=ALU.mult, op1=ALU.add).then_inc(s_row, 1)
            own(ts(prow, prow, flag_b[0:Q, 0:1], None, ALU.mult))
            own(v.scalar_tensor_tensor(out=prow, in0=rawf, scalar=flag_b[0:Q, 2:3], in1=prow, op0=ALU.mult, op1=ALU.add))
            dve.sem_inc(s_row, 3)
            dve.wait_ge(s_bases_st, 16)
            own(v.tensor_copy(base0[:, :, 0:BG], least[:, starts[-1]:starts[-1] + NG].rearrange("o (c g) -> o c g", g=BG)))
            own(v.tensor_copy(iota_run[:], iota[:]))
            dve.sem_inc(w_iota, 1)
            v.tensor_copy(flag[:], flag_f[0:1, 1:2]).then_inc(s_flag, 1)
            dve.wait_ge(s_flag, 1)
            covered = dve.value_load(flag[0:1, 0:1], min_val=0, max_val=1)

            def centre(n, rows, centred):
                own(v.tensor_reduce(stat[0:CP, 0, :], rows3(rows), AX, ALU.add))
                own(ts(stat[0:CP, 0, :], stat[0:CP, 0, :], 1.0 / D, None, ALU.mult))
                v.tensor_tensor(rows3(centred), rows3(rows), wide(stat[0:CP, 0, :]), ALU.subtract).then_inc(s_sq_in, 1)
                dve.wait_ge(s_sq, n + 1)
                v.tensor_reduce(stat[0:CP, 1, :], rows3(sq), AX, ALU.add).then_inc(s_var, 1)
                dve.wait_ge(s_root, n + 1)
                own(v.reciprocal(stat[0:CP, 2, :], stat[0:CP, 2, :]))

            def normed_relu():
                v.scalar_tensor_tensor(out=rows3(hrows), in0=rows3(hrows), scalar=0.0, in1=wide(stat[0:CP, 2, :]),
                                       op0=ALU.max, op1=ALU.mult).then_inc(s_h, 1)

            dve.wait_ge(s_x, 16)
            dve.wait_ge(s_turned, len(pieces))
            centre(0, xrows, hrows)
            normed_relu()
            dve.wait_ge(s_h, 1)
            dve.wait_ge(s_w, 16 * N_W)
            own(v.tensor_tensor(xrows, xrows, hrows, ALU.add))
            v.tensor_tensor(rows3(xrows), rows3(xrows), feat(2), ALU.add).then_inc(s_resid, 1)
            dve.wait_ge(s_resid_st, 16)
            dve.wait_ge(s_ht, NC)
            own(v.memset(deg, 0.0))
            dve.wait_ge(s_clear, 1)
            for done in (s_add0, w_add, s_deg, w_deg, s_dadd):
                dve.sem_inc(done, 1)
            dve.sem_inc(s_add, 2)
            dve.sem_inc(s_cvd, 3)

            def one_hot(slot, values, numbers, done):
                v.tensor_tensor(onehot[:, slot, :, :], numbers[:, :].unsqueeze(1).to_broadcast([P, T, WIN]),
                                values.unsqueeze(2).to_broadcast([P, T, WIN]), ALU.is_equal).then_inc(done, 1)

            def add(at, n, bank, col, done, to=None):
                to = agg_h[0:D, :] if to is None else to
                v.tensor_tensor(to[:, bass.ds(at, n)], to[:, bass.ds(at, n)],
                                ps[bank][0:to.shape[0], col:col + n], ALU.add).then_inc(done, 1)

            def bases_of(row, first, n):
                return nc.values_load_multi_w_load_instructions(
                    row[0:1, bass.ds(first, n)], engines=[mybir.EngineType.DVE], min_val=0, max_val=N - 1,
                    skip_runtime_bounds_check_because="a base is one of dst")[1]

            def all_windows(n, table, with_deg):
                with dve.Fori(0, NG) as g:
                    dve.wait_ge(w_iota, (g + n * NG) * (NWIN + 1) + 1)
                    v.tensor_copy(iota_run[:], iota[:]).then_inc(w_iota, 1)
                    with dve.Fori(0, NWIN) as k:
                        at = (g + n * NG) * NWIN + k
                        dve.wait_ge(w_iota, (g + n * NG) * (NWIN + 1) + k + 2)
                        one_hot(0, table[:, bass.ds(g * T, T)], iota_run, w_oh)
                        dve.wait_ge(w_mm, at + 1)
                        dve.wait_ge(w_add, at + 1)
                        add(k * WIN, WIN, 0, 0, w_add)
                        if with_deg:
                            dve.wait_ge(w_deg, at + 1)
                            add(k * WIN, WIN, 0, WIN, w_deg, deg)
                        dve.wait_ge(w_oh, at + 1)
                        ts(iota_run[:], iota_run[:], float(WIN), None, ALU.add).then_inc(w_iota, 1)
                dve.wait_ge(w_add, (n + 1) * NG * NWIN + 1)
                if with_deg:
                    dve.wait_ge(w_deg, NG * NWIN + 1)

            with dve.If(covered == 1):
                with dve.Fori(0, NIT) as i:
                    for m in range(BODY + LAG):
                        if m < BODY:
                            one_hot(m % OH_SLOTS, rel0[:, bass.ds((i * BODY + m) * T, T)], iota, s_oh)
                        if m < LAG:
                            continue
                        a = m - LAG
                        if a % BG == 0:
                            base = bases_of(bases, (i * (BODY // BG) + a // BG) * 8, BG)
                        dve.wait_ge(s_mm, i * BODY + (a + 1))
                        dve.wait_ge(s_add0, i * BODY + (a + 1))
                        add(base[a % BG], WIN, a % 5, 0, s_add0)
                        dve.wait_ge(s_deg, i * BODY + (a + 1))
                        add(base[a % BG], WIN, a % 5, WIN, s_deg, deg)
                dve.wait_ge(s_add0, NG + 1)
                dve.wait_ge(s_deg, NG + 1)
            with dve.Else():
                all_windows(0, rel0, True)
            dve.sem_inc(s_pass, 1)
            dve.wait_ge(s_ub, 16 * len(regions))
            for r, ub, to in zip(regions, unit_bases, nodes):
                own(v.memset(to, -1.0))
                own(v.tensor_copy(ub, ub.bitcast(I32)))
                low = stat[0:r.blocks, 0, 0:1]
                own(v.tensor_reduce(low, ub[:, 0:r.units], AX, ALU.min))
                own(ts(ub, ub, low, None, ALU.subtract))
                own(v.tensor_tensor(to[:, 0:r.units * r.w].rearrange("b (u d) -> b u d", d=r.w),
                                    ub[:, 0:r.units].unsqueeze(2).to_broadcast([r.blocks, r.units, r.w]),
                                    iota[0:r.blocks, 0:r.w].unsqueeze(1).to_broadcast([r.blocks, r.units, r.w]), ALU.add))
            dve.sem_inc(s_nodes, 1)
            dve.wait_ge(s_deg_ld, 16)
            own(ts(degs[0:CP, :], degs[0:CP, :], 1.0, None, ALU.max))
            v.reciprocal(degs[0:CP, :], degs[0:CP, :]).then_inc(s_dinv, 1)
            dve.wait_ge(s_w, 16 * N_W)
            for k in range(NC):
                dve.wait_ge(s_m3, k + 1)
                v.tensor_tensor(yrows[:, k * J * D:(k + 1) * J * D].rearrange("p (j f) -> p j f", f=D),
                                ps[4 + k % 2][0:CP, 0:J * D].rearrange("p (j f) -> p j f", f=D),
                                brow[0:CP, 0:1, :].to_broadcast([CP, J, D]), ALU.add).then_inc(s_y, 1)
            dve.wait_ge(s_y, NC)
            centre(1, yrows, yrows)
            own(v.tensor_tensor(rows3(yrows), rows3(yrows), wide(stat[0:CP, 2, :]), ALU.mult))
            own(v.tensor_tensor(rows3(yrows), rows3(yrows), feat(1), ALU.mult))
            dve.wait_ge(s_resid_ld, 16)
            own(v.tensor_tensor(yrows, yrows, xrows, ALU.add))
            centre(2, yrows, hrows)
            normed_relu()
            copy_h(dve, v.tensor_copy, 1, range(1, NC, 2))
            dve.wait_ge(s_hi, 1)
            v.tensor_tensor(rows3(xrows), rows3(hrows), parts[:, :, 0, :], ALU.subtract).then_inc(s_t, 1)
            dve.wait_ge(s_mid, 1)
            v.tensor_tensor(parts[:, :, 2, :], rows3(xrows), parts[:, :, 1, :], ALU.subtract).then_inc(s_parts, 1)
            dve.wait_ge(s_parts, 1)
            dve.wait_ge(s_tab, 16)
            dve.wait_ge(s_ht, 2 * NC)
            for c in range(2):
                own(v.memset(counts[c][:, min(r.units * r.w for r in regions):COLS, :], 0.0))
            dve.sem_inc(s_zero, 1)
            dve.wait_ge(s_bases_ld, 16)
            dve.wait_ge(s_node_at, 1)
            dve.wait_ge(s_clear, 2)

            def output_rows(k):
                n = 2 * NC + k
                dve.wait_ge(s_conv, n + 1)
                dve.wait_ge(s_res[k % 2], 16 * (k // 2 + 1))
                stored(dve, n)
                v.tensor_tensor(stage[0:CP, n % STAGES, :], ps[k % 2][0:CP, 0:J * D], resid[0:CP, k % 2, :], ALU.add).then_inc(s_o, 1)

            for layer in range(3):
                def group_one_hot(g, s):
                    one_hot(s, key[:, bass.ds(g * T + TD, T)], iota, s_goh)

                def group_add(g, s, base, blocks):
                    dve.wait_ge(s_win, g + (layer * G + 1 + GSLOT))
                    dve.wait_ge(s_add, g + (layer * G + 2))
                    dve.wait_ge(s_dadd, blocks + (layer * NB + 1))
                    add(base, WIN, WBANK + s % 2, 0, s_add)

                def unit_one_hots(r, b, u, c):
                    nq = len(r.quanta)
                    dve.wait_ge(s_built, b * (r.units * nq) + (r.first_quantum + u * nq + 1))
                    oh = unit_oh[(u + c * r.units) % 2]
                    for t in range(r.k):
                        tile = b * (r.units * r.k) + (r.first_tile + u * r.k + t)
                        ts(oh[:, KW * NR + t * P:KW * NR + t * P + CP], iota16[:, 0:CP], who[:, bass.ds(tile, 1)], None, ALU.is_equal)
                        ins = ts(oh[:, t * r.w * NR:(t + 1) * r.w * NR], iota16[:, 0:r.w * NR], key[:, bass.ds(tile, 1)],
                                 None, ALU.is_equal)
                    ins.then_inc(s_unit, 1)

                def block_add(r, b, groups):
                    dve.wait_ge(s_tr, b + (layer * NB + r.first_block + 2))
                    dve.wait_ge(s_add, groups + (layer * G + 2))
                    dve.wait_ge(s_dadd, b + (layer * NB + r.first_block + 1))
                    base = bases_of(bases, b + (BBASE + r.first_block), 1)[0]
                    add(base, COLS, TURN, 0, s_dadd)

                def selection(r, b):
                    ts(sel[:], iota16[:, 0:COLS], node_at[:, bass.ds(b + r.first_block, 1)], None, ALU.is_equal).then_inc(s_sel, 1)

                def build_step(r, built, multiplied, c):
                    if built is None:
                        selection(r, multiplied)
                        block_add(r, multiplied, 2 * (r.first_block + r.blocks))
                        return
                    g = (built + r.first_block) * 2
                    s = 2 * c
                    blocks = r.first_block if multiplied is None else multiplied + r.first_block
                    for u in range(r.units):
                        unit_one_hots(r, built, u, c)
                        if u == 1:
                            group_one_hot(g + 2, (s + 2) % GSLOT)
                            base = bases_of(bases, g + NBASE, 2)
                            if multiplied is not None:
                                selection(r, multiplied)
                        if u == r.units // 2:
                            group_add(g, s, base[0], blocks)
                            group_one_hot(g + 3, (s + 3) % GSLOT)
                        if u == r.units - 2:
                            group_add(g + 1, s + 1, base[1], blocks)
                            if multiplied is not None:
                                block_add(r, multiplied, g + 2)

                def step(r, built, multiplied, c):
                    if layer == 0:
                        build_step(r, built, multiplied, c)
                        return
                    g = (multiplied + r.first_block) * 2
                    s = 2 * c
                    blocks = multiplied + r.first_block
                    after = next_block(r, multiplied)
                    base = bases_of(bases, g + NBASE, 2)
                    selection(r, multiplied)
                    group_one_hot(g + 2, (s + 2) % GSLOT)
                    if after is not None:
                        to_bf16(dve, layer, after, 1 - c, 0)
                    group_add(g, s, base[0], blocks)
                    group_one_hot(g + 3, (s + 3) % GSLOT)
                    if after is not None:
                        for q in range(1, 3):
                            to_bf16(dve, layer, after, 1 - c, q)
                    group_add(g + 1, s + 1, base[1], blocks)
                    block_add(r, multiplied, g + 2)

                def group(g, s):
                    if not isinstance(g, int) or g + 2 < G:
                        group_one_hot(g + 2, (s + 2) % GSLOT)
                    group_add(g, s, bases_of(bases, g + NBASE, 1)[0], NB)

                with dve.If(covered == 1):
                    for g in range(2):
                        group_one_hot(g, g)
                    if layer > 0:
                        for q in range(3):
                            to_bf16(dve, layer, 0, 0, q)
                    walk(dve, layer, step, group)
                    dve.wait_ge(s_add, (layer + 1) * G + 2)
                    dve.wait_ge(s_dadd, (layer + 1) * NB + 1)
                with dve.Else():
                    all_windows(layer + 1, key, False)
                for step in range(NC + 4):
                    if step < NC:
                        n = layer * NC + step
                        dve.wait_ge(s_dchunk[n % 2], 16 * (n // 2 + 1))
                        v.tensor_tensor(agg_h[0:D, cidx(step)], agg_h[0:D, cidx(step)], dinv[:, n % 2, :], ALU.mult).then_inc(s_scaled, 1)
                    if layer == 2:
                        if 1 <= step <= NC:
                            output_rows(step - 1)
                        continue
                    rows = lambda a: a.rearrange("p (j f) -> p j f", f=D)
                    if 2 <= step < NC + 2:
                        k = step - 2
                        n = layer * NC + k
                        dve.wait_ge(s_hi, 1 + n + 1)
                        if n >= STAGES:
                            dve.wait_ge(s_parts, 1 + n - STAGES + 1)
                        v.tensor_tensor(rows(left[0:CP, n % STAGES, :]), rows(stage[0:CP, n % STAGES, :]),
                                        parts[:, k * J:(k + 1) * J, 0, :], ALU.subtract).then_inc(s_t, 1)
                    if step >= 4:
                        k = step - 4
                        n = layer * NC + k
                        dve.wait_ge(s_mid, 1 + n + 1)
                        v.tensor_tensor(parts[:, k * J:(k + 1) * J, 2, :], rows(left[0:CP, n % STAGES, :]),
                                        parts[:, k * J:(k + 1) * J, 1, :], ALU.subtract).then_inc(s_parts, 1)
                if layer < 2:
                    dve.wait_ge(s_clear, (layer + 1) * NC + 2)


_INS = ['x', 'src', 'dst', 'edge_attr_64', 'L0_gnn_W0', 'L0_gnn_b0', 'L0_gnn_W1', 'L0_gnn_b1', 'L0_gnn_W2', 'L0_gnn_b2',
        'L0_gnn_ln_g', 'L0_gnn_ln_b', 'L1_gnn_W1l', 'L1_gnn_b1', 'L1_gnn_W1r', 'L1_gnn_W2l', 'L1_gnn_b2', 'L1_gnn_W2r',
        'L1_gnn_W3l', 'L1_gnn_b3', 'L1_gnn_W3r']


def kernel(**inputs):
    import concourse.bacc as bacc
    from concourse.bass_utils import run_bass_kernel_spmd

    nc = bacc.Bacc("TRN2", target_bir_lowering=False, num_devices=1)
    arrays, args = {}, []
    for name in _INS:
        a = np.ascontiguousarray(inputs[name])
        arrays[f"in_{name}"] = a
        args.append(nc.dram_tensor(f"in_{name}", a.shape, mybir.dt.from_np(a.dtype), kind="ExternalInput").ap())
    args.append(nc.dram_tensor("out_x", inputs['x'].shape, F32, kind="ExternalOutput").ap())
    gnn_kernel(nc, *args)
    r = run_bass_kernel_spmd(nc, [arrays], core_ids=[0])
    return r.results[0]["out_x"]
```
